# Optimizing a Trainium2 kernel written in Bass

```python
import numpy as np
import jax
import jax.numpy as jnp

def _softmax(x, axis=-1):
    return jax.nn.softmax(x, axis=axis)

def _gelu(x):
    return jax.nn.gelu(x, approximate=True)

def _silu(x):
    return jax.nn.silu(x)

def _sigmoid(x):
    return jax.nn.sigmoid(x)

def _layernorm(x, axis=-1, eps=1e-05):
    m = jnp.mean(x, axis=axis, keepdims=True)
    v = jnp.var(x, axis=axis, keepdims=True)
    return (x - m) / jnp.sqrt(v + eps)

def _scatter_add(tgt, idx, src, axis=0):
    return tgt.at[idx].add(src)

def _segment_sum(src, seg, n):
    return jax.ops.segment_sum(src, seg, n)
kernel_name = 'mk_lm_tower_d1_tok_ids768_r4_c4c8c2'

def setup_inputs(seed: int=0):
    np.random.seed(seed)
    _w = jnp.asarray

    def _rec_inputs():
        import jax
        import jax.numpy as jnp
        _rk = jax.random.key(seed)
        x = jax.random.randint(jax.random.fold_in(_rk, 1), (4, 512), 0, 12564, jnp.int32)
        return x
    x = _rec_inputs()

    def _L0_tok_setup():
        import jax, jax.numpy as jnp
        import numpy as np
        VOCAB = 50257
        DIM = 192
        B, S = (8, 512)
        key = jax.random.key(seed)
        k1, k2 = jax.random.split(key)
        x = jax.random.randint(k1, (B, S), 0, VOCAB, dtype=jnp.int64 if jax.config.jax_enable_x64 else jnp.int32)
        weight = jax.random.normal(k2, (VOCAB, DIM), dtype=jnp.float32)
        return {'x': x, 'weight': weight}
    _L0_tok_all = _L0_tok_setup()
    _L0_tok_in = {k: v for k, v in _L0_tok_all.items() if k in ('weight',)}
    del _L0_tok_all

    def _L0_attn_setup():
        import jax, jax.numpy as jnp
        import numpy as np
        ALPHA = 0.35

        def _round_ln_pow2(x):
            y = jnp.floor(jnp.log2(x))
            up = x - 2.0 ** y > 2.0 ** (y + 1.0) - x
            return 2.0 ** (y + up.astype(x.dtype))
        key = jax.random.key(seed)
        k1, k2, k3, k4, k5 = jax.random.split(key, 5)
        B, N, C = (64, 197, 192)
        return {'x': jax.random.normal(k1, (B, N, C), dtype=jnp.float32), 'qkv_weight': jax.random.normal(k2, (3 * C, C), dtype=jnp.float32) * 0.02, 'qkv_bias': jax.random.normal(k3, (3 * C,), dtype=jnp.float32) * 0.02, 'proj_weight': jax.random.normal(k4, (C, C), dtype=jnp.float32) * 0.02, 'proj_bias': jax.random.normal(k5, (C,), dtype=jnp.float32) * 0.02}
    _L0_attn_all = _L0_attn_setup()
    _L0_attn_in = {k: v for k, v in _L0_attn_all.items() if k in ('qkv_weight', 'qkv_bias', 'proj_weight', 'proj_bias')}
    del _L0_attn_all

    def _L0_ffn_setup():
        import jax, jax.numpy as jnp
        import numpy as np
        B, S, D_IN, D_HID, D_OUT = (32, 128, 192, 768, 192)
        key = jax.random.key(seed)
        k1, k2, k3, k4 = jax.random.split(key, 4)
        init_k = float(np.sqrt(1.0 / D_IN))
        init_k2 = float(np.sqrt(1.0 / D_HID))
        x = jax.random.normal(k1, (B, S, D_IN), dtype=jnp.float32)
        in_weight = jax.random.uniform(k2, (D_HID, D_IN), dtype=jnp.float32, minval=-init_k, maxval=init_k)
        in_bias = jax.random.uniform(k3, (D_HID,), dtype=jnp.float32, minval=-init_k, maxval=init_k)
        out_weight = jax.random.uniform(k4, (D_HID, D_OUT), dtype=jnp.float32, minval=-init_k2, maxval=init_k2)
        return {'x': x, 'in_weight': in_weight, 'in_bias': in_bias, 'out_weight': out_weight}
    _L0_ffn_all = _L0_ffn_setup()
    _L0_ffn_in = {k: v for k, v in _L0_ffn_all.items() if k in ('in_weight', 'in_bias', 'out_weight')}
    del _L0_ffn_all
    return {'x': x, 'L0_tok_weight': _L0_tok_in['weight'], 'L0_attn_qkv_weight': _L0_attn_in['qkv_weight'], 'L0_attn_qkv_bias': _L0_attn_in['qkv_bias'], 'L0_attn_proj_weight': _L0_attn_in['proj_weight'], 'L0_attn_proj_bias': _L0_attn_in['proj_bias'], 'L0_ffn_in_weight': _L0_ffn_in['in_weight'], 'L0_ffn_in_bias': _L0_ffn_in['in_bias'], 'L0_ffn_out_weight': _L0_ffn_in['out_weight']}

def reference(x, L0_tok_weight, L0_attn_qkv_weight, L0_attn_qkv_bias, L0_attn_proj_weight, L0_attn_proj_bias, L0_ffn_in_weight, L0_ffn_in_bias, L0_ffn_out_weight):
    import jax
    import jax.numpy as jnp

    def _L0_tok_ref(x, weight):
        import jax, jax.numpy as jnp
        import numpy as np
        VOCAB = 50257
        DIM = 192
        B, S = (8, 512)
        return weight[x]

    def _L0_attn_ref(x, qkv_weight, qkv_bias, proj_weight, proj_bias):
        import jax, jax.numpy as jnp
        import numpy as np
        ALPHA = 0.35

        def _round_ln_pow2(x):
            y = jnp.floor(jnp.log2(x))
            up = x - 2.0 ** y > 2.0 ** (y + 1.0) - x
            return 2.0 ** (y + up.astype(x.dtype))
        B, N, C = x.shape
        num_heads = 12
        head_dim = C // num_heads
        scale = head_dim ** (-0.5)
        global_max_x = jnp.abs(x).max(axis=(0, 1))
        max_weight = jnp.abs(qkv_weight).max(axis=0)
        channel_scale = _round_ln_pow2(global_max_x ** ALPHA / max_weight ** (1.0 - ALPHA))
        x_smoothed = x / channel_scale[None, None, :]
        weight_smoothed = qkv_weight * channel_scale[None, :]
        h = jnp.einsum('bnc,mc->bnm', x_smoothed, weight_smoothed) + qkv_bias
        qkv = h.reshape(B, N, 3, num_heads, head_dim).transpose(2, 0, 3, 1, 4)
        q, k, v = (qkv[0], qkv[1], qkv[2])
        attn = jnp.einsum('bhnd,bhmd->bhnm', q, k) * scale
        attn = jax.nn.softmax(attn, axis=-1)
        out = jnp.einsum('bhnm,bhmd->bhnd', attn, v)
        out = out.transpose(0, 2, 1, 3).reshape(B, N, C)
        out = jnp.einsum('bnc,mc->bnm', out, proj_weight) + proj_bias
        return out

    def _L0_ffn_ref(x, in_weight, in_bias, out_weight):
        import jax, jax.numpy as jnp
        import numpy as np
        B, S, D_IN, D_HID, D_OUT = (32, 128, 192, 768, 192)
        lead = x.shape[:-1]
        xt = x.reshape(-1, in_weight.shape[1])
        h = jax.nn.gelu(jnp.einsum('td,hd->th', xt, in_weight) + in_bias, approximate=False)
        out = jnp.einsum('th,ho->to', h, out_weight)
        return out.reshape(*lead, out_weight.shape[1])
    h = _L0_tok_ref(x, L0_tok_weight)
    h = h + _L0_attn_ref(_layernorm(h, axis=-1), L0_attn_qkv_weight, L0_attn_qkv_bias, L0_attn_proj_weight, L0_attn_proj_bias)
    h = h + _L0_ffn_ref(_layernorm(h, axis=-1), L0_ffn_in_weight, L0_ffn_in_bias, L0_ffn_out_weight)
    return h

_drawn_inputs = setup_inputs


def setup_inputs(seed=0):
    import zlib

    import numpy as np

    out = dict(_drawn_inputs(seed))
    spreads = {}
    factors = {'L0_attn_qkv_weight': 8.0,
     'L0_attn_qkv_bias': 8.0,
     'L0_attn_proj_weight': 8.0,
     'L0_attn_proj_bias': 10.204,
     'L0_ffn_in_bias': 12.437}
    for name, (base, spread) in spreads.items():
        noise = np.random.default_rng([zlib.crc32(name.encode()), seed]).standard_normal(out[name].shape)
        drawn = base * np.exp(spread * noise) if base else spread * noise
        out[name] = jnp.asarray(drawn.astype(out[name].dtype))
    for name, factor in factors.items():
        out[name] = (out[name] * factor).astype(out[name].dtype)
    return out
```

```python
from contextlib import ExitStack

import concourse.bass as bass
from concourse import mybir

F32 = mybir.dt.float32
BF16 = mybir.dt.bfloat16
I32 = mybir.dt.int32
U32 = mybir.dt.uint32
ALU = mybir.AluOpType
ACT = mybir.ActivationFunctionType
AX = mybir.AxisListType

P = 128
HEADS = 12
ALPHA = 0.35
EPS = 1e-5
FOUR_THIRDS_DOWN = 1.3333332538604736
EXPONENT_BITS = 0x7F800000
HPU = 4
TILE_COLS = 32
PARTS = 3
PRODUCTS = 6
Q_PART = (0, 0, 0, 1, 1, 2)
K_PART = (0, 1, 2, 0, 1, 0)
LEAD = 7


def decoder_layer(nc, x, emb, qkv_w, qkv_b, proj_w, proj_b, ffn_w1, ffn_b1, ffn_w2, out):
    BATCH, SEQ = x.shape
    C = emb.shape[1]
    F = ffn_w1.shape[0]
    HD = C // HEADS
    SCALE = float(HD) ** -0.5
    CH = C // 2
    TT = SEQ // P
    NT = BATCH * TT
    GROUPS = HEADS // HPU
    STACK = PRODUCTS * HD
    ROWS = STACK + PARTS
    KT = TT
    FT = F // P
    UNIT_CH = HPU * HD
    UNITS = BATCH * GROUPS

    qk_parts = nc.dram_tensor("qk_parts", [BATCH, 2, C, PARTS, SEQ], BF16, kind="Internal").ap()
    out_t = out.rearrange("b (p t) c -> b p t c", p=P)

    with ExitStack() as ctx:
        def sb(name, shape, dt=F32):
            return ctx.enter_context(nc.sbuf_tensor(name, shape, dt))

        def sem(name):
            return ctx.enter_context(nc.semaphore(name))

        ps = ctx.enter_context(nc.psum_tensor("ps", [P, 8, 512], F32))

        ids = sb("ids", [P, NT], I32)
        h = sb("h", [P, NT, C])
        z = sb("z", [P, 2, TT, C])
        stats = sb("stats", [P, NT, 6])
        mv = sb("mv", [P, NT, 2])
        rstd = sb("rstd", [P, NT])
        half = sb("half", [P, NT])
        ident = sb("ident", [P, P])
        ident16 = sb("ident16", [P, P], BF16)

        wq_nat = sb("wq_nat", [CH, 6, C])
        wp_nat = sb("wp_nat", [CH, 2, C])
        w1_nat = sb("w1_nat", [P, FT, C])
        qkvT = sb("qkvT", [CH + 1, 2, 3 * C])
        projT = sb("projT", [CH + 1, 2, C])
        w1T = sb("w1T", [CH, 2, F])
        w2 = sb("w2", [P, FT, C])
        b1 = sb("b1", [P, FT])
        qkb = sb("qkb", [CH, 4])
        qkb_s = sb("qkb_s", [CH, 4])

        xT = sb("xT", [CH, 2, BATCH * SEQ])
        xs = sb("xs", [CH + 1, 2, SEQ])
        xmax_b = sb("xmax_b", [CH, 2, BATCH])
        xmax = sb("xmax", [CH, 2])
        wmax = sb("wmax", [CH, 2])
        lnx = sb("lnx", [CH, 2])
        lnw = sb("lnw", [CH, 2])
        lnw65 = sb("lnw65", [CH, 2])
        lns = sb("lns", [CH, 2])
        raw = sb("raw", [CH, 2])
        raw43 = sb("raw43", [CH, 2])
        cs = sb("cs", [CH, 2])
        inv = sb("inv", [CH, 2])

        qk32 = sb("qk32", [CH, 4, SEQ])
        rest = sb("rest", [CH, 4, SEQ])
        parts = sb("parts", [CH, 4, PARTS, SEQ], BF16)
        v_all = sb("v_all", [P, BATCH, KT, HEADS, TILE_COLS])

        QS = [sb(f"QS{g}", [ROWS, HPU, SEQ], BF16) for g in range(GROUPS)]
        KS = [sb(f"KS{g}", [ROWS, HPU, SEQ], BF16) for g in range(GROUPS)]
        VU = [sb(f"VU{g}", [P, KT, HPU, TILE_COLS]) for g in range(GROUPS)]
        negmax = sb("negmax", [P, TT, HPU])
        negrest = sb("negrest", [P, TT, HPU])
        mparts = sb("mparts", [P, TT, PARTS, HPU], BF16)
        mrows = sb("mrows", [PARTS * HPU, SEQ], BF16)
        prob = sb("prob", [P, KT, HPU, SEQ])[:, :, :, :]
        o_sb = sb("o_sb", [P, SEQ])
        rden = sb("rden", [P, TT, HPU])
        attn = sb("attn", [P, UNITS, TT, UNIT_CH])

        a_cur = sb("a_cur", [P, TT, C])
        aT = sb("aT", [CH + 1, 2, SEQ])
        z2T = sb("z2T", [CH, 2, SEQ])
        hid = prob.rearrange("p k h n -> p (k h) n")[:, 0:FT, :]

        ids_in = sem("ids_in")
        gathered = [sem(f"gathered{b}") for b in range(BATCH)]
        wq_in, wp_in, w1_in, small_in, w2_in = (sem(n) for n in ("wq_in", "wp_in", "w1_in", "small_in", "w2_in"))
        consts = sem("consts")
        stats_done, aggr_done, rstd_done, z_done = (sem(n) for n in ("stats_done", "aggr_done", "rstd_done", "z_done"))
        eps_done = sem("eps_done")
        turned, untied = sem("turned"), sem("untied")
        xmax_steps, maxima, logs, lnw_ready, lns_ready = (sem(n) for n in ("xmax_steps", "maxima", "logs", "lnw_ready", "lns_ready"))
        raw_ready, cs_steps, w_scaled = (sem(n) for n in ("raw_ready", "cs_steps", "w_scaled"))
        qkb_ready = sem("qkb_ready")
        xs_ready, qk_mm, qk_taken, v_mm, v_taken = (sem(n) for n in ("xs_ready", "qk_mm", "qk_taken", "v_mm", "v_taken"))
        hi_done, rest_done, mid_done, lo_done = (sem(n) for n in ("hi_done", "rest_done", "mid_done", "lo_done"))
        stored = [sem(f"stored{j}") for j in range(4)]
        qk_in = [sem(f"qk_in{g}") for g in range(GROUPS)]
        m_in = [sem(f"m_in{g}") for g in range(GROUPS)]
        vu_ready = sem("vu_ready")
        a_mm, a_read = sem("a_mm"), sem("a_read")
        m_parts, m_turned, m_taken = (sem(n) for n in ("m_parts", "m_turned", "m_taken"))
        b_mm, p_ready = sem("b_mm"), sem("p_ready")
        pv_done = sem("pv_done")
        o_taken, o_turned, rden_ready, attn_ready = (sem(n) for n in ("o_taken", "o_turned", "rden_ready", "attn_ready"))
        a_copied, a_turned, aT_ready, proj_mm, h1_ready = (sem(n) for n in ("a_copied", "a_turned", "aT_ready", "proj_mm", "h1_ready"))
        stats2, aggr2, eps2, rstd2, z2_done, z_turned, z2T_ready = (sem(n) for n in ("stats2", "aggr2", "eps2", "rstd2", "z2_done", "z_turned", "z2T_ready"))
        f1_mm, gelu_done, f2_mm, y_ready, y_out = (sem(n) for n in ("f1_mm", "gelu_done", "f2_mm", "y_ready", "y_out"))


        def nat(tile, rows, j, c):
            return tile[0:rows, j, c * CH:(c + 1) * CH]

        weight_jobs = [(wq_in, [(nat(wq_nat, CH, j, c), j * CH) for j in range(4)], qkvT[0:CH, c, 0:2 * C])
                       for c in range(2)]
        weight_jobs += [(wq_in, [(nat(wq_nat, CH, 4 + j, c), c * C + j * CH) for c in range(2) for j in range(2)],
                         qkvT[0:CH, :, 2 * C:3 * C])]
        weight_jobs += [(wp_in, [(nat(wp_nat, CH, j, c), c * C + j * CH) for c in range(2) for j in range(2)],
                         projT[0:CH, :, :])]
        weight_jobs += [(w1_in, [(nat(w1_nat, P, 3 * k + j, c), j * P) for j in range(3)],
                         w1T[0:CH, c, 3 * k * P:3 * (k + 1) * P]) for c in range(2) for k in range(2)]
        WJ = len(weight_jobs)

        PAIRS = HPU // 2
        Q_DMAS = 16 * 2 * PRODUCTS
        M_DMAS = 16 * PARTS

        def wait_apart(engine, semaphore, value):
            engine.wait_ge(semaphore, value)
            engine.sem_inc(passed, 1)

        passed = sem("passed")
        block = ctx.enter_context(nc.Block())

        @block.sync
        def _(sp):
            sp.dma_start(ids[:, :].rearrange("p (b t) -> p b t", t=TT), x.rearrange("b (p t) -> p b t", t=TT)).then_inc(ids_in, 16)
            sp.dma_start(wq_nat[:, :, :], qkv_w.rearrange("(j p) c -> p j c", p=CH)).then_inc(wq_in, 16)
            sp.dma_start(wp_nat[:, :, :], proj_w.rearrange("(j p) c -> p j c", p=CH)).then_inc(wp_in, 16)
            sp.dma_start(w1_nat[:, :, :], ffn_w1.rearrange("(j p) c -> p j c", p=P)).then_inc(w1_in, 16)
            sp.dma_start(qkb[:, :], qkv_b[0:2 * C].rearrange("(j p) -> p j", p=CH), allow_slow_non_contiguous=True).then_inc(small_in, 16)
            sp.dma_start(qkvT[CH:CH + 1, 1, 2 * C:3 * C], qkv_b[2 * C:3 * C].rearrange("(a c) -> a c", a=1)).then_inc(small_in, 16)
            sp.dma_start(projT[CH:CH + 1, 1, :], proj_b.rearrange("(a c) -> a c", a=1)).then_inc(small_in, 16)
            sp.dma_start(b1[:, :], ffn_b1.rearrange("(j p) -> p j", p=P), allow_slow_non_contiguous=True).then_inc(small_in, 16)
            sp.dma_start(w2[:, :, :], ffn_w2.rearrange("(j p) c -> p j c", p=P)).then_inc(w2_in, 16)

            with sp.Fori(0, BATCH) as b:
                for j in range(4):
                    sp.wait_ge(lo_done, 4 * b + j + 1)
                    sp.dma_start(qk_parts[bass.ds(b, 1), j // 2, (j % 2) * CH:(j % 2 + 1) * CH, :, :],
                                 parts[:, j, :, :]).then_inc(stored[j], 16)

            def load_unit(b, g):
                for side, stack, part in ((0, QS[g], Q_PART), (1, KS[g], K_PART)):
                    for n in range(PRODUCTS):
                        src = qk_parts[bass.ds(b, 1), side, g * UNIT_CH:(g + 1) * UNIT_CH, part[n], :]
                        sp.dma_start(stack[n * HD:(n + 1) * HD, :, :],
                                     src.rearrange("o (h d) n -> d (o h) n", d=HD)).then_inc(qk_in[g], 16)

            for j in range(4):
                sp.wait_ge(stored[j], 16 * BATCH)
            for g in range(GROUPS):
                load_unit(0, g)
            with sp.Fori(1, BATCH) as b:
                for g in range(GROUPS):
                    sp.wait_ge(b_mm, PAIRS * KT * (GROUPS * (b - 1) + g + 1))
                    load_unit(b, g)

            with sp.Fori(0, BATCH) as b:
                sp.wait_ge(y_ready, 2 + 2 * b + 2)
                sp.dma_start(out_t[bass.ds(b, 1), :, :, :].rearrange("o p t c -> p (o t) c"),
                             h[:, bass.ds(TT * b, TT), :]).then_inc(y_out, 16)
            sp.wait_ge(y_out, 16 * BATCH)

        @block.gpsimd
        def _(gp):
            gp.wait_ge(ids_in, 16)

            def gather(b):
                for t in range(b * TT, (b + 1) * TT):
                    gp.indirect_dma_start(
                        out=h[:, t, :], out_offset=None, in_=emb[:, :],
                        in_offset=bass.IndirectOffsetOnAxis(ap=ids[:, t:t + 1], axis=0),
                    ).then_inc(gathered[b], 16)

            def rstd_of(b):
                here = slice(b * TT, (b + 1) * TT)
                gp.wait_ge(aggr_done, TT * (b + 1))
                gp.tensor_scalar(rstd[:, here], mv[:, here, 1], EPS, None, ALU.add).then_inc(eps_done, 1)
                gp.wait_ge(eps_done, b + 1)
                gp.tensor_tensor(rstd[:, here], rstd[:, here], half[:, here], ALU.pow).then_inc(rstd_done, 1)

            gather(0)
            gp.memset(ident[:, :], 0.0).then_inc(consts, 1)
            gp.memset(ident16[:, :], 0.0).then_inc(consts, 1)
            gp.memset(half[:, :], -0.5).then_inc(consts, 1)
            gp.wait_ge(consts, 3)
            for m in (ident, ident16):
                gp.affine_select(out=m[:, :], in_=m[:, :], compare_op=ALU.not_equal, fill=1.0,
                                 base=0, pattern=[[-1, P]], channel_multiplier=1).then_inc(consts, 1)
            gather(1)
            rstd_of(0)
            gather(2)
            rstd_of(1)
            gather(3)
            rstd_of(2)
            rstd_of(3)
            gp.memset(v_all[:, :, :, :, HD:TILE_COLS], 0.0).then_inc(consts, 1)
            gp.wait_ge(consts, 6)
            gp.memset(xs[CH:CH + 1, :, :], 1.0).then_inc(consts, 1)
            gp.wait_ge(consts, 7)
            gp.memset(aT[CH:CH + 1, :, :], 1.0).then_inc(consts, 1)
            for g in range(GROUPS):
                gp.wait_ge(consts, 8 + g)
                gp.memset(KS[g][STACK:ROWS, :, :], 1.0).then_inc(consts, 1)
            gp.wait_ge(consts, 11)
            gp.memset(v_all[:, :, :, :, HD:HD + 1], 1.0).then_inc(consts, 1)

            def copy_v(b, g):
                gp.tensor_copy(VU[g][:, :, :, :],
                               v_all[:, bass.ds(b, 1), :, g * HPU:(g + 1) * HPU, :].rearrange(
                                   "p o t h c -> p (o t) h c")).then_inc(vu_ready, 1)

            gp.wait_ge(v_taken, TT * BATCH)
            gp.wait_ge(consts, 12)
            for g in range(GROUPS):
                copy_v(0, g)
            with gp.Fori(1, BATCH) as b:
                for g in range(GROUPS):
                    gp.wait_ge(pv_done, KT + KT * (GROUPS * (b - 1) + g + 1))
                    copy_v(b, g)

            gp.wait_ge(attn_ready, 1 + UNITS)

            def front(b):
                gp.tensor_copy(a_cur[:, :, :].rearrange("p t (g c) -> p g t c", g=GROUPS),
                               attn[:, bass.ds(GROUPS * b, GROUPS), :, :]).then_inc(a_copied, 1)
                wait_apart(gp, aggr2, TT * b + TT)
                gp.tensor_scalar(rstd[:, 0:TT], mv[:, 0:TT, 1], EPS, None, ALU.add).then_inc(eps2, 1)
                gp.wait_ge(eps2, b + 1)
                gp.tensor_tensor(rstd[:, 0:TT], rstd[:, 0:TT], half[:, 0:TT], ALU.pow).then_inc(rstd2, 1)

            front(0)
            with gp.Fori(1, BATCH) as b:
                gp.wait_ge(a_turned, 2 * b)
                gp.wait_ge(z2_done, TT * b)
                front(b)

        @block.scalar
        def _(act):
            for n, (_, _, dst) in enumerate(weight_jobs):
                cols = 1
                for d in dst.shape[1:]:
                    cols *= d
                src = ps[0:CH, 4 + n % 4, 0:cols]
                if len(dst.shape) == 3:
                    src = src.rearrange("p (c n) -> p c n", c=2)
                act.wait_ge(turned, n + 1)
                act.activation(dst, src, ACT.Copy).then_inc(untied, 1)
            for k in range(2 * BATCH):
                b, c = k // 2, k % 2
                act.wait_ge(turned, WJ + k + 1)
                act.activation(xT[:, c, b * SEQ:(b + 1) * SEQ], ps[0:CH, k % 4, :], ACT.Copy).then_inc(untied, 1)

            act.wait_ge(maxima, 2)
            act.activation(lnx[:, :], xmax[:, :], ACT.Ln).then_inc(logs, 1)
            act.activation(lnw[:, :], wmax[:, :], ACT.Ln).then_inc(logs, 1)
            act.wait_ge(lns_ready, 1)
            act.activation(raw[:, :], lns[:, :], ACT.Exp).then_inc(raw_ready, 1)

            act.wait_ge(qkb_ready, 2)
            act.wait_ge(consts, 12)

            def qkv_out(b, first=False):
                for j in range(4):
                    scale = SCALE if j < 2 else 1.0
                    act.wait_ge(qk_mm, 4 * b + j + 1)
                    if not first:
                        act.wait_ge(lo_done, 4 * (b - 1) + j + 1)
                        act.wait_ge(stored[j], 16 * b)
                    act.activation(qk32[:, j, :], ps[0:CH, j, :], ACT.Identity, bias=qkb_s[:, j:j + 1],
                                   scale=scale).then_inc(qk_taken, 1)
                    act.activation(parts[:, j, 0, :], ps[0:CH, j, :], ACT.Identity, bias=qkb_s[:, j:j + 1],
                                   scale=scale).then_inc(hi_done, 1)
                for t in range(TT):
                    act.wait_ge(v_mm, TT * b + t + 1)
                    act.activation(v_all[:, bass.ds(b, 1), t, :, 0:HD].rearrange("p o h d -> p (o h) d"),
                                   ps[:, 4 + t, 0:C].rearrange("p (h d) -> p h d", d=HD),
                                   ACT.Copy).then_inc(v_taken, 1)

            qkv_out(0, first=True)
            with act.Fori(1, BATCH) as b:
                qkv_out(b)

            def exps(step, kt):
                for pair in range(PAIRS):
                    act.wait_ge(b_mm, PAIRS * step + pair + 1)
                    if pair == 0:
                        act.wait_ge(pv_done, step + 1)
                    act.activation(prob[:, kt, 2 * pair:2 * pair + 2, :],
                                   ps[:, 2 + 2 * pair:4 + 2 * pair, :], ACT.Exp).then_inc(p_ready, 1)

            def max_rows(b, g, first=False):
                act.wait_ge(m_turned, GROUPS * b + g + 1)
                if not first:
                    before = (b, g - 1) if g else (b - 1, GROUPS - 1)
                    act.wait_ge(m_in[before[1]], M_DMAS * (before[0] + 1))
                act.activation(mrows[:, :], ps[0:PARTS * HPU, 7, :].bitcast(BF16)[:, 0:SEQ],
                               ACT.Copy).then_inc(m_taken, 1)
                act.wait_ge(m_taken, GROUPS * b + g + 1)
                for n in range(PARTS):
                    act.dma_start(QS[g][STACK + n:STACK + n + 1, :, :], mrows[n * HPU:(n + 1) * HPU, :]).then_inc(m_in[g], 16)

            def out_copy(unit):
                act.wait_ge(pv_done, KT + KT * (unit + 1))
                act.wait_ge(o_turned, 1 + unit)
                act.activation(o_sb[:, :], ps[:, 6, :], ACT.Copy).then_inc(o_taken, 1)

            max_rows(0, 0, first=True)
            exps(0, 0)

            def unit_exps(b, g, last=False):
                unit = GROUPS * b + g
                exps(KT * unit + 1, 1)
                exps(KT * unit + 2, 2)
                if not last:
                    nb, ng = (b, g + 1) if g + 1 < GROUPS else (b + 1, 0)
                    max_rows(nb, ng)
                exps(KT * unit + 3, 3)
                if not last:
                    exps(KT * unit + 4, 0)
                out_copy(unit)

            with act.Fori(0, BATCH - 1) as b:
                for g in range(GROUPS):
                    unit_exps(b, g)
            for g in range(GROUPS):
                unit_exps(BATCH - 1, g, last=g == GROUPS - 1)

            def attn_T(b):
                for c in range(2):
                    act.wait_ge(a_turned, 2 * b + c + 1)
                    act.activation(aT[0:CH, c, :], ps[0:CH, c, :], ACT.Copy).then_inc(aT_ready, 1)

            def z_T(b):
                for c in range(2):
                    act.wait_ge(z_turned, 2 * b + c + 1)
                    act.activation(z2T[:, c, :], ps[0:CH, c, :], ACT.Copy).then_inc(z2T_ready, 1)

            def gelus(b):
                for m in range(FT):
                    act.wait_ge(f1_mm, FT * b + m + 1)
                    act.activation(hid[:, m, :], ps[:, 4 + m % 2, :], ACT.Gelu, bias=b1[:, m:m + 1]).then_inc(gelu_done, 1)

            attn_T(0)
            z_T(0)
            with act.Fori(0, BATCH - 1) as b:
                gelus(b)
                attn_T(b + 1)
                z_T(b + 1)
            gelus(BATCH - 1)

        @block.vector
        def _(dve):
            for b in range(BATCH):
                here = range(b * TT, (b + 1) * TT)
                dve.wait_ge(gathered[b], 16 * TT)
                for t in here:
                    dve.bn_stats(stats[:, t, :], h[:, t, :]).then_inc(stats_done, 1)
                dve.wait_ge(stats_done, (b + 1) * TT)
                for t in here:
                    dve.bn_aggr(mv[:, t, :], stats[:, t, :]).then_inc(aggr_done, 1)
                if b == 1:
                    dve.wait_ge(untied, 3)
                    dve.tensor_reduce(wmax[:, :], qkvT[0:CH, :, :], AX.X, ALU.max,
                                      apply_absolute_value=True).then_inc(maxima, 1)
                dve.wait_ge(rstd_done, b + 1)
                if b >= 2:
                    dve.wait_ge(turned, WJ + 2 * (b - 1))
                for t in here:
                    dve.tensor_scalar(z[:, b % 2, t % TT, :], h[:, t, :], mv[:, t, 0:1], rstd[:, t:t + 1],
                                      ALU.subtract, ALU.mult).then_inc(z_done, 1)
            for b in range(BATCH):
                dve.wait_ge(untied, WJ + 2 * (b + 1))
                dve.tensor_reduce(xmax_b[:, :, b], xT[:, :, b * SEQ:(b + 1) * SEQ], AX.X, ALU.max,
                                  apply_absolute_value=True).then_inc(xmax_steps, 1)
            dve.wait_ge(xmax_steps, BATCH)
            dve.tensor_reduce(xmax[:, :], xmax_b[:, :, :], AX.X, ALU.max).then_inc(maxima, 1)
            dve.wait_ge(small_in, 64)
            dve.tensor_scalar(qkb_s[:, 0:2], qkb[:, 0:2], SCALE, None, ALU.mult).then_inc(qkb_ready, 1)
            dve.tensor_copy(qkb_s[:, 2:4], qkb[:, 2:4]).then_inc(qkb_ready, 1)
            dve.wait_ge(logs, 2)
            dve.tensor_scalar(lnw65[:, :], lnw[:, :], 1.0 - ALPHA, None, ALU.mult).then_inc(lnw_ready, 1)
            dve.wait_ge(lnw_ready, 1)
            dve.scalar_tensor_tensor(lns[:, :], lnx[:, :], ALPHA, lnw65[:, :], ALU.mult, ALU.subtract).then_inc(lns_ready, 1)
            dve.wait_ge(raw_ready, 1)
            dve.tensor_scalar(raw43[:, :], raw[:, :], FOUR_THIRDS_DOWN, None, ALU.mult).then_inc(cs_steps, 1)
            dve.wait_ge(cs_steps, 1)
            dve.tensor_scalar(cs[:, :].bitcast(U32), raw43[:, :].bitcast(U32), EXPONENT_BITS, None,
                              ALU.bitwise_and).then_inc(cs_steps, 1)
            dve.wait_ge(cs_steps, 2)
            dve.reciprocal(inv[:, :], cs[:, :]).then_inc(cs_steps, 1)
            dve.wait_ge(cs_steps, 3)
            for c in range(2):
                dve.tensor_scalar(qkvT[0:CH, c, :], qkvT[0:CH, c, :], cs[:, c:c + 1], None, ALU.mult).then_inc(w_scaled, 1)

            def smooth(b):
                for c in range(2):
                    dve.tensor_scalar(xs[0:CH, c, :], xT[:, c, bass.ds(SEQ * b, SEQ)], inv[:, c:c + 1], None,
                                      ALU.mult).then_inc(xs_ready, 1)

            def split(b):
                for j in range(4):
                    n = 4 * b + j + 1
                    dve.wait_ge(qk_taken, n)
                    dve.wait_ge(hi_done, n)
                    dve.tensor_tensor(rest[:, j, :], qk32[:, j, :], parts[:, j, 0, :], ALU.subtract).then_inc(rest_done, 1)
                    dve.wait_ge(rest_done, n)
                    dve.tensor_copy(parts[:, j, 1, :], rest[:, j, :]).then_inc(mid_done, 1)
                    dve.wait_ge(mid_done, n)
                    dve.tensor_tensor(parts[:, j, 2, :], rest[:, j, :], parts[:, j, 1, :], ALU.subtract).then_inc(lo_done, 1)

            smooth(0)
            with dve.Fori(1, BATCH) as b:
                split(b - 1)
                dve.wait_ge(v_mm, TT * b)
                smooth(b)
            split(BATCH - 1)

            def maximum(unit):
                for n in range(HPU * TT):
                    head, t = n // TT, n % TT
                    dve.wait_ge(a_mm, HPU * TT * unit + n + 1)
                    dve.tensor_reduce(negmax[:, t, head:head + 1], ps[:, n % 2, :], AX.X, ALU.max,
                                      negate=True).then_inc(a_read, 1)
                dve.wait_ge(a_read, HPU * TT * (unit + 1))
                dve.wait_ge(m_turned, unit)
                dve.tensor_copy(mparts[:, :, 0, :], negmax[:, :, :]).then_inc(m_parts, 1)
                dve.wait_ge(m_parts, 4 * unit + 1)
                dve.tensor_tensor(negrest[:, :, :], negmax[:, :, :], mparts[:, :, 0, :], ALU.subtract).then_inc(m_parts, 1)
                dve.wait_ge(m_parts, 4 * unit + 2)
                dve.tensor_copy(mparts[:, :, 1, :], negrest[:, :, :]).then_inc(m_parts, 1)
                dve.wait_ge(m_parts, 4 * unit + 3)
                dve.tensor_tensor(mparts[:, :, 2, :], negrest[:, :, :], mparts[:, :, 1, :], ALU.subtract).then_inc(m_parts, 1)

            def normalise(unit):
                o = ps[:, 7, :].rearrange("p (t h c) -> p t h c", t=TT, h=HPU)
                dve.wait_ge(o_turned, 1 + unit + 1)
                dve.reciprocal(rden[:, :, :], o[:, :, :, HD:HD + 1].rearrange("p t h o -> p t (h o)")).then_inc(rden_ready, 1)
                dve.wait_ge(rden_ready, unit + 1)
                dve.tensor_tensor(
                    attn[:, bass.ds(unit, 1), :, :].rearrange("p o t (h d) -> p (o t) h d", d=HD), o[:, :, :, 0:HD],
                    rden[:, :, :].unsqueeze(3).broadcast_to([P, TT, HPU, HD]), ALU.mult).then_inc(attn_ready, 1)

            maximum(0)
            maximum(1)
            with dve.Fori(0, UNITS - 2) as unit:
                maximum(unit + 2)
                normalise(unit)
            normalise(UNITS - 2)
            normalise(UNITS - 1)

            def residual_and_norm(b):
                for i in range(2):
                    rows = h[:, bass.ds(TT * b + 2 * i, 2), :]
                    dve.wait_ge(proj_mm, 2 * b + i + 1)
                    dve.tensor_tensor(rows, ps[:, 2 + i, :].rearrange("p (t c) -> p t c", t=2)[:, :, 0:C], rows,
                                      ALU.add).then_inc(h1_ready, 1)
                wait_apart(dve, h1_ready, 2 * b + 2)
                for t in range(TT):
                    dve.bn_stats(stats[:, t, :], h[:, bass.ds(TT * b + t, 1), :].rearrange("p o c -> p (o c)")).then_inc(stats2, 1)
                wait_apart(dve, stats2, TT * b + TT)
                for t in range(TT):
                    dve.bn_aggr(mv[:, t, :], stats[:, t, :]).then_inc(aggr2, 1)
                dve.wait_ge(rstd2, b + 1)
                for t in range(TT):
                    dve.tensor_scalar(z[:, 0, t, :], h[:, bass.ds(TT * b + t, 1), :].rearrange("p o c -> p (o c)"),
                                      mv[:, t, 0:1], rstd[:, t:t + 1], ALU.subtract, ALU.mult).then_inc(z2_done, 1)

            def result(b, i):
                rows = h[:, bass.ds(TT * b + 2 * i, 2), :]
                dve.wait_ge(f2_mm, 2 * b + i + 1)
                dve.tensor_tensor(rows, ps[:, 6 + i, :].rearrange("p (t c) -> p t c", t=2)[:, :, 0:C], rows,
                                  ALU.add).then_inc(y_ready, 1)

            residual_and_norm(0)
            with dve.Fori(0, BATCH - 1) as b:
                result(b, 0)
                residual_and_norm(b + 1)
                result(b, 1)
            result(BATCH - 1, 0)
            result(BATCH - 1, 1)

        @block.tensor
        def _(pe):
            mm = pe.matmul

            pe.wait_ge(consts, 5)
            for n, (loaded, tiles, _) in enumerate(weight_jobs):
                pe.wait_ge(loaded, 16)
                if n >= 4:
                    pe.wait_ge(untied, n - 3)
                for src, col in tiles:
                    rows = src.shape[0]
                    last = pe.transpose(ps[0:CH, 4 + n % 4, col:col + rows], src, ident[0:rows, 0:rows])
                last.then_inc(turned, 1)
            for b in range(BATCH):
                pe.wait_ge(z_done, TT * (b + 1))
                for c in range(2):
                    k = 2 * b + c
                    if k >= 4:
                        pe.wait_ge(untied, WJ + k - 3)
                    for t in range(TT):
                        last = pe.transpose(ps[0:CH, k % 4, t * P:(t + 1) * P],
                                            z[:, b % 2, t, c * CH:(c + 1) * CH], ident[:, :])
                    last.then_inc(turned, 1)

            pe.wait_ge(w_scaled, 2)
            pe.wait_ge(small_in, 64)
            pe.wait_ge(consts, 7)
            pe.wait_ge(untied, WJ + 2 * BATCH)

            def qkv(b, first=False):
                pe.wait_ge(xs_ready, 2 * b + 2)
                for j in range(4):
                    if not first:
                        pe.wait_ge(hi_done, 4 * (b - 1) + j + 1)
                    for c in range(2):
                        last = mm(ps[0:CH, j, :], qkvT[0:CH, c, j * CH:(j + 1) * CH], xs[0:CH, c, :],
                                  start=c == 0, stop=c == 1)
                    last.then_inc(qk_mm, 1)
                for t in range(TT):
                    if not first:
                        pe.wait_ge(v_taken, TT * (b - 1) + t + 1)
                    tok = slice(t * P, (t + 1) * P)
                    mm(ps[:, 4 + t, 0:C], xs[0:CH, 0, tok], qkvT[0:CH, 0, 2 * C:3 * C], start=True, stop=False)
                    mm(ps[:, 4 + t, 0:C], xs[0:CH + 1, 1, tok], qkvT[0:CH + 1, 1, 2 * C:3 * C],
                       start=False, stop=True).then_inc(v_mm, 1)

            qkv(0, first=True)
            with pe.Fori(1, BATCH) as b:
                qkv(b)

            pe.wait_ge(hi_done, 4 * BATCH)
            pe.wait_ge(v_taken, TT * BATCH)
            pe.wait_ge(consts, 11)
            pe.nop().then_inc(pv_done, KT)
            pe.nop().then_inc(o_turned, 1)
            pe.nop().then_inc(attn_ready, 1)
            pe.nop().then_inc(y_ready, 2)

            def scores_for_max(b, g, head, chunk, tiles, first=False):
                if head == 0 and 0 in tiles:
                    pe.wait_ge(qk_in[g], Q_DMAS * (b + 1))
                for t in tiles:
                    if not (first and t < 2):
                        pe.wait_ge(a_read, TT * chunk + t - 1)
                    mm(ps[:, t % 2, :], QS[g][0:STACK, head, t * P:(t + 1) * P], KS[g][0:STACK, head, :],
                       start=True, stop=True).then_inc(a_mm, 1)

            def turn_max(unit):
                pe.wait_ge(m_parts, 4 * unit + 4)
                pe.wait_ge(attn_ready, 1 if isinstance(unit, int) and unit == 0 else unit)
                for t in range(TT):
                    last = pe.transpose(ps[0:PARTS * HPU, 7, :].bitcast(BF16)[:, t * P:(t + 1) * P],
                                        mparts[:, t, :, :].rearrange("p a h -> p (a h)"), ident16[:, :])
                last.then_inc(m_turned, 1)

            def scores(b, g, kt, step, pairs=range(PAIRS), first=False):
                if kt == 0 and 0 in pairs:
                    pe.wait_ge(m_in[g], M_DMAS * (b + 1))
                for pair in pairs:
                    if not first:
                        pe.wait_ge(p_ready, PAIRS * (step - 1) + pair + 1)
                    for head in (2 * pair, 2 * pair + 1):
                        last = mm(ps[:, 2 + head, :], KS[g][:, head, kt * P:(kt + 1) * P], QS[g][:, head, :],
                                  start=True, stop=True)
                    last.then_inc(b_mm, 1)

            def weigh(unit, g, kt, first=False):
                pe.wait_ge(p_ready, PAIRS * (KT * unit + kt + 1))
                if kt == 0:
                    pe.wait_ge(vu_ready, unit + 1)
                    pe.wait_ge(o_taken, unit)
                for head in range(HPU):
                    last = mm(ps[head * TILE_COLS:(head + 1) * TILE_COLS, 6, :], VU[g][:, kt, head, :],
                              prob[:, kt, head, :], start=kt == 0, stop=kt == KT - 1)
                last.then_inc(pv_done, 1)

            def turn_out(unit, final=False):
                pe.wait_ge(o_taken, unit + 1)
                pe.wait_ge(m_taken, unit + 2 - final)
                pe.wait_ge(attn_ready, 1 + unit)
                for t in range(TT):
                    last = pe.transpose(ps[:, 7, t * P:(t + 1) * P], o_sb[:, t * P:(t + 1) * P], ident[:, :])
                last.then_inc(o_turned, 1)

            def at(b, g, steps):
                return b + (g + steps) // GROUPS, (g + steps) % GROUPS

            def chunk(b, g, ahead, tiles=range(TT), first=False):
                nb, ng = at(b, g, ahead // HPU)
                if isinstance(nb, int) and nb >= BATCH:
                    return
                scores_for_max(nb, ng, ahead % HPU, HPU * (GROUPS * b + g) + ahead, tiles, first)

            def step(b, g, kt):
                unit = GROUPS * b + g
                nb, ng = at(b, g, (kt + 1) // KT)
                more = not (isinstance(nb, int) and nb == BATCH)
                for pair in range(PAIRS):
                    if more:
                        scores(nb, ng, (kt + 1) % KT, KT * unit + kt + 1, (pair,))
                    chunk(b, g, LEAD + kt, (pair,))
                if kt == 1 and not (isinstance(b, int) and unit == UNITS - 1):
                    turn_max(unit + 1)
                chunk(b, g, LEAD + kt, (2,))
                weigh(unit, g, kt)
                chunk(b, g, LEAD + kt, (3,))

            def unit_steps(b, g):
                unit = GROUPS * b + g
                final = isinstance(b, int) and unit == UNITS - 1
                for kt in range(1, KT):
                    step(b, g, kt)
                if not final:
                    nb, ng = at(b, g, 1)
                    step(nb, ng, 0)
                turn_out(unit, final)

            for n in range(HPU):
                chunk(0, 0, n, first=n == 0)
            turn_max(0)
            for n in range(HPU, LEAD):
                chunk(0, 0, n)
            scores(0, 0, 0, 0, first=True)
            step(0, 0, 0)
            with pe.Fori(0, BATCH - 1) as b:
                for g in range(GROUPS):
                    unit_steps(b, g)
            for g in range(GROUPS):
                unit_steps(BATCH - 1, g)

            def turn_attn(b):
                pe.wait_ge(a_copied, b + 1)
                for c in range(2):
                    for t in range(TT):
                        last = pe.transpose(ps[0:CH, c, t * P:(t + 1) * P], a_cur[:, t, c * CH:(c + 1) * CH], ident[:, :])
                    last.then_inc(a_turned, 1)

            def project(b):
                pe.wait_ge(aT_ready, 2 * b + 2)
                for t in range(TT):
                    to, tok = ps[:, 2 + t // 2, (t % 2) * 256:(t % 2) * 256 + C], slice(t * P, (t + 1) * P)
                    mm(to, aT[0:CH, 0, tok], projT[0:CH, 0, :], start=True, stop=False)
                    last = mm(to, aT[:, 1, tok], projT[:, 1, :], start=False, stop=True)
                    if t % 2:
                        last.then_inc(proj_mm, 1)

            def turn_z(b):
                pe.wait_ge(z2_done, TT * (b + 1))
                for c in range(2):
                    for t in range(TT):
                        last = pe.transpose(ps[0:CH, c, t * P:(t + 1) * P], z[:, 0, t, c * CH:(c + 1) * CH], ident[:, :])
                    last.then_inc(z_turned, 1)

            def ffn1(b):
                pe.wait_ge(z2T_ready, 2 * b + 2)
                for m in range(FT):
                    if m >= 2:
                        pe.wait_ge(gelu_done, FT * b + m - 1)
                    for c in range(2):
                        last = mm(ps[:, 4 + m % 2, :], w1T[:, c, m * P:(m + 1) * P], z2T[:, c, :],
                                  start=c == 0, stop=c == 1)
                    last.then_inc(f1_mm, 1)

            def ffn2(b, i):
                if i == 0:
                    pe.wait_ge(gelu_done, FT * (b + 1))
                    pe.wait_ge(y_ready, 2 + 2 * b)
                for t in (2 * i, 2 * i + 1):
                    for m in range(FT):
                        last = mm(ps[:, 6 + i, (t % 2) * 256:(t % 2) * 256 + C], hid[:, m, t * P:(t + 1) * P],
                                  w2[:, m, :], start=m == 0, stop=m == FT - 1)
                last.then_inc(f2_mm, 1)

            pe.wait_ge(w2_in, 16)
            pe.wait_ge(consts, 8)
            turn_attn(0)
            project(0)
            turn_z(0)
            with pe.Fori(0, BATCH - 1) as b:
                ffn1(b)
                turn_attn(b + 1)
                ffn2(b, 0)
                project(b + 1)
                ffn2(b, 1)
                turn_z(b + 1)
            ffn1(BATCH - 1)
            ffn2(BATCH - 1, 0)
            ffn2(BATCH - 1, 1)


_INS = ['x', 'L0_tok_weight', 'L0_attn_qkv_weight', 'L0_attn_qkv_bias', 'L0_attn_proj_weight', 'L0_attn_proj_bias',
        'L0_ffn_in_weight', 'L0_ffn_in_bias', 'L0_ffn_out_weight']


def kernel(**inputs):
    import numpy as _np
    import concourse.bacc as _bacc
    from concourse import mybir as _mybir
    from concourse.bass_utils import run_bass_kernel_spmd as _run

    nc = _bacc.Bacc("TRN2", target_bir_lowering=False, num_devices=1)
    arrays, args = {}, []
    for name in _INS:
        a = _np.ascontiguousarray(inputs[name])
        arrays[f"in_{name}_dram"] = a
        args.append(nc.dram_tensor(f"in_{name}_dram", a.shape, _mybir.dt.from_np(a.dtype), kind="ExternalInput").ap())
    shape = (*inputs['x'].shape, inputs['L0_tok_weight'].shape[1])
    args.append(nc.dram_tensor("out_0_dram", shape, _mybir.dt.float32, kind="ExternalOutput").ap())
    decoder_layer(nc, *args)
    r = _run(nc, [arrays], core_ids=[0])
    return r.results[0]["out_0_dram"]
```

```python
from contextlib import ExitStack

import concourse.bass as bass
from concourse import mybir

F32 = mybir.dt.float32
F32R = mybir.dt.float32r
BF16 = mybir.dt.bfloat16
I32 = mybir.dt.int32
U32 = mybir.dt.uint32
ALU = mybir.AluOpType
ACT = mybir.ActivationFunctionType
AX = mybir.AxisListType

P = 128
HEADS = 12
ALPHA = 0.35
EPS = 1e-5
FOUR_THIRDS_DOWN = 1.3333332538604736
EXPONENT_BITS = 0x7F800000
HPU = 4
TILE_COLS = 32
PARTS = 3
PRODUCTS = 7
Q_PART = (0, 0, 0, 1, 1, 1, 2)
K_PART = (0, 1, 2, 0, 1, 2, 0)
Q_RUNS = ((0, 3, 0, 0), (3, 3, 1, 0), (6, 1, 2, 0))
K_RUNS = ((0, 3, 0, 1), (3, 3, 0, 1), (6, 1, 0, 0))
LEAD = 7


def decoder_layer(nc, x, emb, qkv_w, qkv_b, proj_w, proj_b, ffn_w1, ffn_b1, ffn_w2, out):
    BATCH, SEQ = x.shape
    C = emb.shape[1]
    F = ffn_w1.shape[0]
    HD = C // HEADS
    SCALE = float(HD) ** -0.5
    CH = C // 2
    CB = C - P
    WIDE = P + 2 * CB
    TT = SEQ // P
    NT = BATCH * TT
    GROUPS = HEADS // HPU
    STACK = PRODUCTS * HD
    ROWS = STACK + PARTS
    KT = TT
    FT = F // P
    UNIT_CH = HPU * HD
    UNITS = BATCH * GROUPS

    BLOCKS = (((0, 0), (0, 1)), ((1, 0), (1, 1)), ((0, 2), (1, 2)))
    QKT = len(BLOCKS)
    qk_parts = nc.dram_tensor("qk_parts", [BATCH, QKT, PARTS, P, SEQ], BF16, kind="Internal").ap()
    out_t = out.rearrange("b (p t) c -> b p t c", p=P)

    with ExitStack() as ctx:
        def sb(name, shape, dt=F32):
            return ctx.enter_context(nc.sbuf_tensor(name, shape, dt))

        def sem(name):
            return ctx.enter_context(nc.semaphore(name))

        ps = ctx.enter_context(nc.psum_tensor("ps", [P, 8, 512], F32))

        ids = sb("ids", [P, NT], I32)
        h = sb("h", [P, NT, C])
        z = sb("z", [P, 2, TT, WIDE])
        stats = sb("stats", [P, NT, 6])
        mv = sb("mv", [P, NT, 2])
        rstd = sb("rstd", [P, NT])
        minus_half = sb("minus_half", [P, TT])
        eps = sb("eps", [P, 1])
        root = sb("root", [P, NT])
        ident = sb("ident", [P, P])
        ident16 = sb("ident16", [P, P], BF16)

        prob = sb("prob", [P, KT, HPU, SEQ])

        def borrow(kt, at, *shape):
            room = prob[:, kt:kt + 2, :, :].rearrange("p k h n -> p (k h n)")
            return room[:, at:at + shape[0] * shape[1]].rearrange("p (a b) -> p a b", a=shape[0])

        wq_nat = borrow(0, 0, QKT, WIDE)
        w1_nat = borrow(0, QKT * WIDE, FT, WIDE)
        wv_nat = borrow(0, (QKT + FT) * WIDE, 2, WIDE)[0:CH]
        wp_nat = borrow(0, (QKT + FT + 2) * WIDE, 2, WIDE)[0:CH]
        qk32, rest = borrow(2, 0, QKT, SEQ), borrow(2, QKT * SEQ, QKT, SEQ)
        qkvT = [sb(f"qkvT_{n}", [P, 2, 3 * C], F32R) for n in ("hi", "lo")]
        projT = [sb(f"projT_{n}", [P, 2, C], F32R) for n in ("hi", "lo")]
        w1T = [sb(f"w1T_{n}", [P, 2, F], F32R) for n in ("hi", "lo")]
        w2 = sb("w2", [P, FT, C])
        w2s = [sb(f"w2_{n}", [P, FT, C], F32R) for n in ("hi", "lo")]
        vbias = sb("vbias", [P, C])
        pbias = sb("pbias", [P, C])
        X = [[sb(f"X{i}_{n}", [P, SEQ], F32R) for n in ("hi", "lo", "both")] for i in range(2)]
        b1 = sb("b1", [P, FT])
        qkb = sb("qkb", [P, QKT])
        qkb_s = sb("qkb_s", [P, QKT])
        qk_scale = sb("qk_scale", [P, QKT])

        xT = sb("xT", [P, 2, BATCH * SEQ])
        attn = xT[:, :, :].rearrange("p a (b c) -> p (a b) c", c=UNIT_CH)[:, 0:UNITS * TT, :].rearrange(
            "p (u t) c -> p u t c", u=UNITS)
        xmax_b = sb("xmax_b", [P, 2, BATCH])
        xmax = sb("xmax", [P, 2])
        wmax_p = sb("wmax_p", [P, 2, 2])
        wmax = sb("wmax", [P, 2])
        powers = sb("powers", [P, 2, 2])
        xpow = sb("xpow", [P, 2])
        wpow = sb("wpow", [P, 2])
        raw = sb("raw", [P, 2])
        raw43 = sb("raw43", [P, 2])
        cs = sb("cs", [P, 2])
        inv = sb("inv", [P, 2])

        parts = sb("parts", [P, 2, QKT, PARTS, SEQ], BF16)
        room = parts[:, :, :, :, :].rearrange("p a b c n -> p (a b c n)").bitcast(F32)
        a_cur = room[:, 0:TT * WIDE].rearrange("p (t c) -> p t c", t=TT)
        hid32 = room[:, TT * WIDE:TT * WIDE + 2 * SEQ].rearrange("p (m n) -> p m n", m=2)
        v_all = sb("v_all", [P, BATCH, KT, C])

        QS = [sb(f"QS{g}", [ROWS, HPU, SEQ], BF16) for g in range(GROUPS)]
        KS = [sb(f"KS{g}", [ROWS, HPU, SEQ], BF16) for g in range(GROUPS)]
        VU = [sb(f"VU{g}", [P, KT, HPU, TILE_COLS]) for g in range(GROUPS)]
        negmax = sb("negmax", [P, TT, HPU])
        negrest = sb("negrest", [P, TT, HPU])
        mparts = sb("mparts", [P, TT, PARTS, HPU], BF16)
        mrows = sb("mrows", [PARTS * HPU, SEQ], BF16)
        o_sb = z[:, 1, 0:2, :].rearrange("p t c -> p (t c)")
        rden = sb("rden", [P, TT, HPU])

        hid = [sb(f"hid_{n}", [P, FT, SEQ], F32R) for n in ("hi", "lo")]
        newton = sb("newton", [P, 3, NT])

        ids_in = sem("ids_in")
        gathered = [sem(f"gathered{b}") for b in range(BATCH)]
        wq_in, wp_in, w1_in, small_in, w2_in = (sem(n) for n in ("wq_in", "wp_in", "w1_in", "small_in", "w2_in"))
        consts = sem("consts")
        stats_done, aggr_done, rstd_steps, z_done = (sem(n) for n in ("stats_done", "aggr_done", "rstd_steps", "z_done"))
        root_done, wv_in = sem("root_done"), sem("wv_in")
        w_hi_done, w_lo_done, bias_added = sem("w_hi_done"), sem("w_lo_done"), sem("bias_added")
        wmax_steps, w2_hi_done, w2_lo_done, doubled = (sem(n) for n in ("wmax_steps", "w2_hi_done", "w2_lo_done", "doubled"))
        turned, untied = sem("turned"), sem("untied")
        xmax_steps, xmax_ready, wmax_ready = (sem(n) for n in ("xmax_steps", "xmax_ready", "wmax_ready"))
        xpow_ready, wpow_ready, cs_steps, w_scaled = (sem(n) for n in ("xpow_ready", "wpow_ready", "cs_steps", "w_scaled"))
        filled = sem("filled")
        qkb_ready = sem("qkb_ready")
        x_hi_done, x_lo_done, qk_mm, qk_taken, v_mm, v_taken = (sem(n) for n in ("x_hi_done", "x_lo_done", "qk_mm", "qk_taken", "v_mm", "v_taken"))
        hi_done, rest_done, mid_done, lo_done = (sem(n) for n in ("hi_done", "rest_done", "mid_done", "lo_done"))
        stored = [[sem(f"stored{i}_{j}") for j in range(QKT)] for i in range(2)]
        qk_in = [sem(f"qk_in{g}") for g in range(GROUPS)]
        m_in = [sem(f"m_in{g}") for g in range(GROUPS)]
        vu_ready = sem("vu_ready")
        a_mm, a_read = sem("a_mm"), sem("a_read")
        m_parts, m_turned, m_taken = (sem(n) for n in ("m_parts", "m_turned", "m_taken"))
        b_mm, p_ready = sem("b_mm"), sem("p_ready")
        pv_done = sem("pv_done")
        o_taken, o_turned, rden_ready, attn_ready = (sem(n) for n in ("o_taken", "o_turned", "rden_ready", "attn_ready"))
        a_copied, a_turned, aT_hi, aT_lo, proj_mm, h1_ready = (sem(n) for n in ("a_copied", "a_turned", "aT_hi", "aT_lo", "proj_mm", "h1_ready"))
        stats2, aggr2, eps2, rstd2, z2_done, z_turned, zT_hi, zT_lo = (sem(n) for n in ("stats2", "aggr2", "eps2", "rstd2", "z2_done", "z_turned", "zT_hi", "zT_lo"))
        f1_mm, gelu_done, hid_hi, hid_lo, f2_mm, y_ready, y_out = (sem(n) for n in ("f1_mm", "gelu_done", "hid_hi", "hid_lo", "f2_mm", "y_ready", "y_out"))


        def nat(tile, rows, j, c):
            return tile[0:rows, j, c * P:(c + 1) * P]

        weight_jobs = [(wq_in, 96, [(nat(wq_nat, P, j, c), j * P) for j in range(QKT)], qkvT, c, 0) for c in range(2)]
        weight_jobs += [(wv_in, 16, [(nat(wv_nat, CH, j, c), c * C + j * CH) for c in range(2) for j in range(2)],
                         qkvT, None, 2 * C)]
        weight_jobs += [(wp_in, 16, [(nat(wp_nat, CH, j, c), c * C + j * CH) for c in range(2) for j in range(2)],
                         projT, None, 0)]
        weight_jobs += [(w1_in, 16, [(nat(w1_nat, P, 3 * k + j, c), j * P) for j in range(3)], w1T, c, 3 * k * P)
                        for c in range(2) for k in range(2)]
        JOB_COLS = 3 * P

        def job_views(n):
            _, _, _, dst, c, col = weight_jobs[n]
            bank = ps[:, 4 + n % 4, 0:JOB_COLS]
            if c is None:
                return (bank.rearrange("p (c n) -> p c n", c=2), *(d[:, :, col:col + C] for d in dst))
            return (bank, *(d[:, c, col:col + JOB_COLS] for d in dst))

        WJ = len(weight_jobs)

        PAIRS = HPU // 2
        Q_DMAS = 16 * (len(Q_RUNS) + len(K_RUNS))
        M_DMAS = 16 * PARTS
        EARLY = ((0,) * (QKT + TT), (0,) * (QKT + TT), (0, 0, 0, 0, 0, 1, 1), (3, 3, 3, 2, 2, 2, 2))

        def wait_apart(engine, semaphore, value):
            engine.wait_ge(semaphore, value)
            engine.sem_inc(passed, 1)

        passed = sem("passed")
        block = ctx.enter_context(nc.Block())

        @block.sync
        def _(sp):
            sp.dma_start(ids[:, :].rearrange("p (b t) -> p b t", t=TT), x.rearrange("b (p t) -> p b t", t=TT)).then_inc(ids_in, 16)
            for tile, halves in enumerate(BLOCKS):
                for half, (side, g) in enumerate(halves):
                    row = side * C + g * UNIT_CH
                    sp.dma_start(wq_nat[half * UNIT_CH:(half + 1) * UNIT_CH, tile, 0:C],
                                 qkv_w[row:row + UNIT_CH, :].rearrange("(h d) c -> d h c", d=HD)).then_inc(wq_in, 16)
            sp.dma_start(wv_nat[:, :, 0:C], qkv_w[2 * C:3 * C, :].rearrange("(j p) c -> p j c", p=CH)).then_inc(wv_in, 16)
            sp.dma_start(wp_nat[:, :, 0:C], proj_w.rearrange("(j p) c -> p j c", p=CH)).then_inc(wp_in, 16)
            sp.dma_start(w1_nat[:, :, 0:C], ffn_w1.rearrange("(j p) c -> p j c", p=P)).then_inc(w1_in, 16)
            for tile, halves in enumerate(BLOCKS):
                for half, (side, g) in enumerate(halves):
                    row = side * C + g * UNIT_CH
                    sp.dma_start(qkb[half * UNIT_CH:(half + 1) * UNIT_CH, tile:tile + 1],
                                 qkv_b[row:row + UNIT_CH].rearrange("(h d o) -> d h o", d=HD, o=1),
                                 allow_slow_non_contiguous=True).then_inc(small_in, 16)
            sp.dma_start(vbias[:, :], qkv_b[2 * C:3 * C].rearrange("(a c) -> a c", a=1).broadcast_to([P, C])).then_inc(small_in, 16)
            sp.dma_start(pbias[:, :], proj_b.rearrange("(a c) -> a c", a=1).broadcast_to([P, C])).then_inc(small_in, 16)
            sp.dma_start(b1[:, :], ffn_b1.rearrange("(j p) -> p j", p=P), allow_slow_non_contiguous=True).then_inc(small_in, 16)
            sp.dma_start(w2[:, :, :], ffn_w2.rearrange("(j p) c -> p j c", p=P)).then_inc(w2_in, 16)

            def store_parts(b, tiles=range(QKT)):
                for tile in tiles:
                    sp.wait_ge(lo_done, QKT * b + tile + 1)
                    sp.dma_start(qk_parts[b, tile].rearrange("n r s -> r n s"), parts[:, b % 2, tile, :, :]).then_inc(stored[b % 2][tile], 16)

            def load_unit(b, g):
                for to, side, (n, count, first, step) in [(QS[g], 0, run) for run in Q_RUNS] + [(KS[g], 1, run) for run in K_RUNS]:
                    tile, half = next((i, j) for i in range(QKT) for j in range(2) if BLOCKS[i][j] == (side, g))
                    rows = slice(half * UNIT_CH, (half + 1) * UNIT_CH)
                    last = first + (count if step else 1)
                    piece = qk_parts[bass.ds(b, 1), tile, first:last, rows, :].rearrange(
                        "o n (d h) s -> (o n) d (h s)", d=HD).broadcast_to([count, HD, HPU * SEQ])
                    sp.dma_start(to[n * HD:(n + count) * HD, :, :].rearrange("r h s -> r (h s)"), piece).then_inc(qk_in[g], 16)

            store_parts(0, (0, 1))
            sp.wait_ge(filled, 11)
            sp.wait_ge(stored[0][0], 16)
            sp.wait_ge(stored[0][1], 16)
            load_unit(0, 0)
            store_parts(0, (2,))
            store_parts(1)
            load_unit(0, 1)
            store_parts(2)
            sp.wait_ge(stored[0][2], 16)
            load_unit(0, 2)
            store_parts(3)
            for tile in range(QKT):
                for buffer in stored:
                    sp.wait_ge(buffer[tile], 16 * BATCH // 2)
            with sp.Fori(1, BATCH) as b:
                for g in range(GROUPS):
                    sp.wait_ge(b_mm, PAIRS * KT * (GROUPS * (b - 1) + g + 1))
                    load_unit(b, g)

            with sp.Fori(0, BATCH) as b:
                sp.wait_ge(y_ready, 2 + 2 * b + 2)
                sp.dma_start(out_t[bass.ds(b, 1), :, :, :].rearrange("o p t c -> p (o t) c"),
                             h[:, bass.ds(TT * b, TT), :]).then_inc(y_out, 16)
            sp.wait_ge(y_out, 16 * BATCH)

        @block.gpsimd
        def _(gp):
            gp.wait_ge(ids_in, 16)

            def gather(b):
                for t in range(b * TT, (b + 1) * TT):
                    gp.indirect_dma_start(
                        out=h[:, t, :], out_offset=None, in_=emb[:, :],
                        in_offset=bass.IndirectOffsetOnAxis(ap=ids[:, t:t + 1], axis=0),
                    ).then_inc(gathered[b], 16)

            gather(0)
            gp.memset(ident[:, :], 0.0).then_inc(consts, 1)
            gp.memset(ident16[:, :], 0.0).then_inc(consts, 1)
            gp.wait_ge(consts, 2)
            for m in (ident, ident16):
                gp.affine_select(out=m[:, :], in_=m[:, :], compare_op=ALU.not_equal, fill=1.0,
                                 base=0, pattern=[[-1, P]], channel_multiplier=1).then_inc(consts, 1)
            gather(1)
            gather(2)
            gather(3)
            gp.wait_ge(wmax_ready, 1)
            gp.wait_ge(filled, 4)
            gp.tensor_tensor(wpow[:, :], wmax[:, :], powers[:, 1, :], ALU.pow).then_inc(wpow_ready, 1)
            gp.wait_ge(xmax_ready, 1)
            gp.tensor_tensor(xpow[:, :], xmax[:, :], powers[:, 0, :], ALU.pow).then_inc(xpow_ready, 1)

            for n in range(QKT * BATCH):
                b, tile = n // QKT, n % QKT
                gp.wait_ge(mid_done, n + 1)
                gp.tensor_tensor(parts[:, b % 2, tile, 2, :], rest[:, tile, :], parts[:, b % 2, tile, 1, :], ALU.subtract).then_inc(lo_done, 1)

            def copy_v(b, g):
                chs = slice(g * UNIT_CH, (g + 1) * UNIT_CH)
                gp.tensor_tensor(
                    VU[g][:, :, :, 0:HD],
                    v_all[:, bass.ds(b, 1), :, chs].rearrange("p o t (h c) -> p (o t) h c", c=HD),
                    vbias[:, chs].rearrange("p (h c) -> p h c", c=HD).unsqueeze(1).broadcast_to([P, KT, HPU, HD]),
                    ALU.add).then_inc(vu_ready, 1)

            gp.wait_ge(v_taken, TT * BATCH)
            gp.wait_ge(filled, 17)
            for g in range(GROUPS):
                copy_v(0, g)
            gp.wait_ge(z_done, 2 * NT)
            gp.tensor_tensor(h[:, :, :], h[:, :, :], pbias[:, :].unsqueeze(1).broadcast_to([P, NT, C]),
                             ALU.add).then_inc(bias_added, 1)
            gp.wait_ge(w2_in, 16)
            gp.tensor_copy(w2s[0][:, :, :], w2[:, :, :]).then_inc(w2_hi_done, 1)
            gp.wait_ge(w2_hi_done, 1)
            gp.tensor_tensor(w2s[1][:, :, :], w2[:, :, :], w2s[0][:, :, :].bitcast(F32), ALU.subtract).then_inc(w2_lo_done, 1)
            with gp.Fori(1, BATCH) as b:
                for g in range(GROUPS):
                    gp.wait_ge(pv_done, KT + KT * (GROUPS * (b - 1) + g + 1))
                    copy_v(b, g)

            def rstd_of(b):
                wait_apart(gp, aggr2, TT * b + TT)
                gp.tensor_scalar(rstd[:, 0:TT], mv[:, 0:TT, 1], EPS, None, ALU.add).then_inc(eps2, 1)
                gp.wait_ge(eps2, b + 1)
                gp.tensor_tensor(rstd[:, 0:TT], rstd[:, 0:TT], minus_half[:, 0:TT], ALU.pow).then_inc(rstd2, 1)

            rstd_of(0)
            with gp.Fori(1, BATCH) as b:
                gp.wait_ge(z2_done, 2 * TT * b)
                rstd_of(b)

        @block.scalar
        def _(act):
            def roots(b):
                here = slice(b * TT, (b + 1) * TT)
                act.wait_ge(aggr_done, TT * (b + 1))
                act.activation(root[:, here], mv[:, here, 1], ACT.Sqrt, bias=eps[:, 0:1]).then_inc(root_done, 1)

            act.wait_ge(filled, 1)
            for n in range(WJ):
                bank, hi, _ = job_views(n)
                act.wait_ge(turned, n + 1)
                act.activation(hi, bank, ACT.Copy).then_inc(w_hi_done, 1)
            roots(0)
            for b in range(BATCH):
                if b + 1 < BATCH:
                    roots(b + 1)
                for k in (2 * b, 2 * b + 1):
                    act.wait_ge(turned, WJ + k + 1)
                    act.activation(xT[:, k % 2, b * SEQ:(b + 1) * SEQ], ps[:, k % 4, :], ACT.Copy).then_inc(untied, 1)

            act.wait_ge(qkb_ready, 1)
            act.wait_ge(filled, 17)

            def smooth_hi(b):
                if b >= 2:
                    act.wait_ge(v_mm, TT * (b - 1))
                for c, to in ((0, X[b % 2][0]), (1, X[b % 2][2])):
                    act.activation(to[:, :], xT[:, c, b * SEQ:(b + 1) * SEQ], ACT.Copy,
                                   scale=inv[:, c:c + 1]).then_inc(x_hi_done, 1)

            def max_rows(b, g, first=False):
                act.wait_ge(m_turned, GROUPS * b + g + 1)
                if not first:
                    before = (b, g - 1) if g else (b - 1, GROUPS - 1)
                    act.wait_ge(m_in[before[1]], M_DMAS * (before[0] + 1))
                act.activation(mrows[:, :], ps[0:PARTS * HPU, 7, :].bitcast(BF16)[:, 0:SEQ],
                               ACT.Copy).then_inc(m_taken, 1)
                act.wait_ge(m_taken, GROUPS * b + g + 1)
                for n in range(PARTS):
                    act.dma_start(QS[g][STACK + n:STACK + n + 1, :, :], mrows[n * HPU:(n + 1) * HPU, :]).then_inc(m_in[g], 16)

            def qkv_out(b, first=False):
                for tile in range(QKT):
                    act.wait_ge(qk_mm, QKT * b + tile + 1)
                    if not first:
                        act.wait_ge(lo_done, QKT * (b - 1) + tile + 1)
                    if b >= 2:
                        act.wait_ge(stored[b % 2][tile], 16 * (b // 2))
                    act.activation(qk32[:, tile, :], ps[:, 2 + tile, :], ACT.Identity, bias=qkb_s[:, tile:tile + 1],
                                   scale=qk_scale[:, tile:tile + 1]).then_inc(qk_taken, 1)
                    act.activation(parts[:, b % 2, tile, 0, :], ps[:, 2 + tile, :], ACT.Identity, bias=qkb_s[:, tile:tile + 1],
                                   scale=qk_scale[:, tile:tile + 1]).then_inc(hi_done, 1)
                for t in range(TT):
                    act.wait_ge(v_mm, TT * b + t + 1)
                    act.activation(v_all[:, b, t, :], ps[:, 5 + t % 3, 0:C], ACT.Copy).then_inc(v_taken, 1)

            act.wait_ge(cs_steps, 5)
            smooth_hi(0)
            for b in range(BATCH):
                if b + 1 < BATCH:
                    smooth_hi(b + 1)
                qkv_out(b, first=b == 0)
            max_rows(0, 0, first=True)

            def exps(step, kt):
                for pair in range(PAIRS):
                    act.wait_ge(b_mm, PAIRS * step + pair + 1)
                    if pair == 0:
                        act.wait_ge(pv_done, step + 1)
                    act.activation(prob[:, kt, 2 * pair:2 * pair + 2, :],
                                   ps[:, 2 + 2 * pair:4 + 2 * pair, :], ACT.Exp).then_inc(p_ready, 1)

            def out_copy(unit):
                act.wait_ge(pv_done, KT + KT * (unit + 1))
                act.wait_ge(o_turned, 1 + unit)
                act.activation(o_sb[:, :], ps[:, 6, :], ACT.Copy).then_inc(o_taken, 1)

            exps(0, 0)

            def unit_exps(b, g, last=False):
                unit = GROUPS * b + g
                exps(KT * unit + 1, 1)
                exps(KT * unit + 2, 2)
                if not last:
                    nb, ng = (b, g + 1) if g + 1 < GROUPS else (b + 1, 0)
                    max_rows(nb, ng)
                exps(KT * unit + 3, 3)
                if not last:
                    exps(KT * unit + 4, 0)
                out_copy(unit)

            with act.Fori(0, BATCH - 1) as b:
                for g in range(GROUPS):
                    unit_exps(b, g)
            for g in range(GROUPS):
                unit_exps(BATCH - 1, g, last=g == GROUPS - 1)

            def copy_attn(b):
                rows = attn[:, bass.ds(GROUPS * b, GROUPS), :, :].rearrange("p g t c -> p t g c")
                act.activation(a_cur[:, :, 0:P].rearrange("p t (g c) -> p t g c", g=2), rows[:, :, 0:2, :],
                               ACT.Copy).then_inc(a_copied, 1)
                act.activation(a_cur[:, :, P:WIDE].rearrange("p t (g c) -> p t g c", g=2),
                               rows[:, :, 2:3, :].broadcast_to([P, TT, 2, CB]), ACT.Copy).then_inc(a_copied, 1)

            def high(b, buffer, ready, done):
                for c, to in ((0, buffer[0]), (1, buffer[2])):
                    act.wait_ge(ready, 2 * b + c + 1)
                    act.activation(to[:, :], ps[:, c, :], ACT.Copy).then_inc(done, 1)

            def gelus(b):
                for m in range(FT):
                    act.wait_ge(f1_mm, FT * b + m + 1)
                    act.wait_ge(hid_lo, FT * b + m + 1)
                    act.activation(hid32[:, m % 2, :], ps[:, 4 + m % 2, :], ACT.Gelu, bias=b1[:, m:m + 1]).then_inc(gelu_done, 1)

            def act_batch(b, last=False):
                high(b + 1, X[0], a_turned, aT_hi)
                gelus(b)
                if not last:
                    copy_attn(b + 2)
                high(b + 1, X[1], z_turned, zT_hi)

            act.wait_ge(attn_ready, 1 + UNITS)
            copy_attn(0)
            high(0, X[0], a_turned, aT_hi)
            copy_attn(1)
            high(0, X[1], z_turned, zT_hi)
            with act.Fori(0, BATCH - 2) as b:
                act_batch(b)
            act_batch(BATCH - 2, last=True)
            gelus(BATCH - 1)

        @block.vector
        def _(dve):
            dve.memset(eps[:, :], EPS).then_inc(filled, 1)
            dve.memset(minus_half[:, :], -0.5).then_inc(filled, 1)
            dve.memset(powers[:, 0, :], ALPHA).then_inc(filled, 1)
            dve.memset(powers[:, 1, :], ALPHA - 1.0).then_inc(filled, 1)
            for g in range(GROUPS):
                dve.memset(KS[g][3 * 32:ROWS, :, :], 1.0).then_inc(filled, 1)
                dve.memset(VU[g][:, :, :, HD:TILE_COLS], 0.0).then_inc(filled, 1)
            dve.wait_ge(filled, 10)
            for g in range(GROUPS):
                dve.memset(VU[g][:, :, :, HD:HD + 1], 1.0)
            dve.memset(newton[:, 2, :], 0.0).then_inc(filled, 1)
            for tile, halves in enumerate(BLOCKS):
                for half, (side, _) in enumerate(halves):
                    dve.memset(qk_scale[half * UNIT_CH:(half + 1) * UNIT_CH, tile:tile + 1],
                               1.0 if side else SCALE).then_inc(filled, 1)

            for tile, loaded, count in ((wq_nat, wq_in, 96), (wv_nat, wv_in, 16), (wp_nat, wp_in, 16), (w1_nat, w1_in, 16)):
                dve.wait_ge(loaded, count)
                dve.tensor_copy(tile[:, :, C:WIDE], tile[:, :, P:C]).then_inc(doubled, 1)

            def normal(to, rows, t, done):
                dve.tensor_scalar(to[:, 0:P], rows[:, 0:P], mv[:, t, 0:1], rstd[:, t:t + 1],
                                  ALU.subtract, ALU.mult).then_inc(done, 1)
                dve.tensor_scalar(to[:, P:WIDE].rearrange("p (a c) -> p a c", a=2),
                                  rows[:, P:C].unsqueeze(1).broadcast_to([P, 2, CB]), mv[:, t, 0:1], rstd[:, t:t + 1],
                                  ALU.subtract, ALU.mult).then_inc(done, 1)

            def low_weights(n):
                bank, hi, lo = job_views(n)
                dve.wait_ge(w_hi_done, n + 1)
                if n < 2:
                    dve.tensor_reduce(wmax_p[:, 0, n:n + 1], bank, AX.X, ALU.max,
                                      apply_absolute_value=True).then_inc(wmax_steps, 1)
                if n == 2:
                    dve.tensor_reduce(wmax_p[:, 1, :], bank, AX.X, ALU.max,
                                      apply_absolute_value=True).then_inc(wmax_steps, 1)
                dve.tensor_tensor(lo, bank, hi.bitcast(F32), ALU.subtract).then_inc(w_lo_done, 1)

            def largest(b):
                dve.wait_ge(untied, 2 * (b + 1))
                dve.tensor_reduce(xmax_b[:, :, b], xT[:, :, b * SEQ:(b + 1) * SEQ], AX.X, ALU.max,
                                  apply_absolute_value=True).then_inc(xmax_steps, 1)

            for n in range(WJ):
                low_weights(n)
            for b in range(BATCH):
                here = range(b * TT, (b + 1) * TT)
                dve.wait_ge(gathered[b], 16 * TT)
                for t in here:
                    dve.bn_stats(stats[:, t, :], h[:, t, :]).then_inc(stats_done, 1)
                dve.wait_ge(stats_done, (b + 1) * TT)
                for t in here:
                    dve.bn_aggr(mv[:, t, :], stats[:, t, :]).then_inc(aggr_done, 1)
                y, v = rstd[:, b * TT:(b + 1) * TT], newton[:, 0, b * TT:(b + 1) * TT]
                e = newton[:, 1, b * TT:(b + 1) * TT]
                dve.wait_ge(aggr_done, TT * (b + 1))
                dve.tensor_scalar(v, mv[:, b * TT:(b + 1) * TT, 1], EPS, None, ALU.add).then_inc(rstd_steps, 1)
                dve.wait_ge(root_done, b + 1)
                dve.reciprocal(y, root[:, b * TT:(b + 1) * TT]).then_inc(rstd_steps, 1)
                dve.wait_ge(rstd_steps, 5 * b + 2)
                dve.tensor_tensor(e, v, y, ALU.mult).then_inc(rstd_steps, 1)
                dve.wait_ge(rstd_steps, 5 * b + 3)
                dve.scalar_tensor_tensor(e, e, -0.5, y, ALU.mult, ALU.mult).then_inc(rstd_steps, 1)
                dve.wait_ge(rstd_steps, 5 * b + 4)
                dve.scalar_tensor_tensor(y, e, 1.5, y, ALU.add, ALU.mult).then_inc(rstd_steps, 1)
                dve.wait_ge(rstd_steps, 5 * b + 5)
                if b >= 2:
                    dve.wait_ge(turned, WJ + 2 * (b - 1))
                for t in here:
                    normal(z[:, b % 2, t % TT, :], h[:, t, :], t, z_done)
                if b == 0:
                    dve.wait_ge(wmax_steps, 3)
                    dve.tensor_tensor(wmax[:, :], wmax_p[:, 0, :], wmax_p[:, 1, :], ALU.max).then_inc(wmax_ready, 1)
                    dve.wait_ge(small_in, 16 * 9)
                    dve.tensor_tensor(qkb_s[:, :], qkb[:, :], qk_scale[:, :], ALU.mult).then_inc(qkb_ready, 1)
                else:
                    largest(b - 1)
            largest(BATCH - 1)
            dve.wait_ge(xmax_steps, BATCH)
            dve.tensor_reduce(xmax[:, :], xmax_b[:, :, :], AX.X, ALU.max).then_inc(xmax_ready, 1)
            dve.wait_ge(wpow_ready, 1)
            dve.wait_ge(xpow_ready, 1)
            dve.tensor_tensor(raw[:, :], xpow[:, :], wpow[:, :], ALU.mult).then_inc(cs_steps, 1)
            dve.wait_ge(cs_steps, 1)
            dve.tensor_scalar(raw43[:, :], raw[:, :], FOUR_THIRDS_DOWN, None, ALU.mult).then_inc(cs_steps, 1)
            dve.wait_ge(cs_steps, 2)
            dve.tensor_scalar(cs[:, :].bitcast(U32), raw43[:, :].bitcast(U32), EXPONENT_BITS, None,
                              ALU.bitwise_and).then_inc(cs_steps, 1)
            dve.wait_ge(cs_steps, 3)
            dve.reciprocal(inv[:, :], cs[:, :]).then_inc(cs_steps, 2)
            dve.wait_ge(cs_steps, 5)

            def row_maximum(n, head, t):
                dve.wait_ge(a_mm, n + 1)
                dve.tensor_reduce(negmax[:, t, head:head + 1], ps[:, t % 2, :], AX.X, ALU.max,
                                  negate=True).then_inc(a_read, 1)

            def split_maximum(unit):
                dve.wait_ge(a_read, HPU * TT * (unit + 1))
                if not (isinstance(unit, int) and unit == 0):
                    dve.wait_ge(m_turned, unit)
                dve.tensor_copy(mparts[:, :, 0, :], negmax[:, :, :]).then_inc(m_parts, 1)
                dve.wait_ge(m_parts, 4 * unit + 1)
                dve.tensor_tensor(negrest[:, :, :], negmax[:, :, :], mparts[:, :, 0, :], ALU.subtract).then_inc(m_parts, 1)
                dve.wait_ge(m_parts, 4 * unit + 2)
                dve.tensor_copy(mparts[:, :, 1, :], negrest[:, :, :]).then_inc(m_parts, 1)
                dve.wait_ge(m_parts, 4 * unit + 3)
                dve.tensor_tensor(mparts[:, :, 2, :], negrest[:, :, :], mparts[:, :, 1, :], ALU.subtract).then_inc(m_parts, 1)

            def smooth_lo(b):
                hi, lo, both = X[b % 2]
                tokens = slice(b * SEQ, (b + 1) * SEQ)
                dve.wait_ge(x_hi_done, 2 * b + 1)
                dve.scalar_tensor_tensor(lo[:, :], xT[:, 0, tokens], inv[:, 0:1], hi[:, :].bitcast(F32),
                                         ALU.mult, ALU.subtract).then_inc(x_lo_done, 1)
                dve.wait_ge(x_hi_done, 2 * b + 2)
                dve.scalar_tensor_tensor(both[CB:P, :], xT[CB:P, 1, tokens], inv[CB:P, 1:2],
                                         both[CB:P, :].bitcast(F32), ALU.mult, ALU.subtract).then_inc(x_lo_done, 1)

            for c in range(2):
                for part in qkvT:
                    dve.tensor_scalar(part[:, c, :], part[:, c, :].bitcast(F32), cs[:, c:c + 1], None,
                                      ALU.mult).then_inc(w_scaled, 1)
                if c == 0:
                    smooth_lo(0)

            def split(b, tile):
                n = QKT * b + tile + 1
                dve.wait_ge(qk_taken, n)
                dve.wait_ge(hi_done, n)
                dve.tensor_tensor(rest[:, tile, :], qk32[:, tile, :], parts[:, b % 2, tile, 0, :], ALU.subtract).then_inc(rest_done, 1)
                dve.wait_ge(rest_done, n)
                dve.tensor_copy(parts[:, b % 2, tile, 1, :], rest[:, tile, :]).then_inc(mid_done, 1)

            def chunk_maximum(chunk):
                for t in range(TT):
                    row_maximum(TT * chunk + t, chunk % HPU, t)

            def early_maxima(n, count):
                for i in range(n, n + count):
                    row_maximum(i, i // TT % HPU, i % TT)
                    if i == HPU * TT - 1:
                        split_maximum(0)
                return n + count

            early = 0
            for b in range(BATCH):
                if b + 1 < BATCH:
                    smooth_lo(b + 1)
                for tile in range(QKT):
                    split(b, tile)
                    early = early_maxima(early, EARLY[b][tile])
                early = early_maxima(early, sum(EARLY[b][QKT:]))
            early_maxima(early, LEAD * TT - early)

            def normalise(unit):
                o = ps[:, 7, :].rearrange("p (t h c) -> p t h c", t=TT, h=HPU)
                dve.wait_ge(o_turned, 1 + unit + 1)
                dve.reciprocal(rden[:, :, :], o[:, :, :, HD:HD + 1].rearrange("p t h o -> p t (h o)")).then_inc(rden_ready, 1)
                dve.wait_ge(rden_ready, unit + 1)
                dve.tensor_tensor(
                    attn[:, bass.ds(unit, 1), :, :].rearrange("p o t (h d) -> p (o t) h d", d=HD), o[:, :, :, 0:HD],
                    rden[:, :, :].unsqueeze(3).broadcast_to([P, TT, HPU, HD]), ALU.mult).then_inc(attn_ready, 1)

            chunk_maximum(LEAD)
            split_maximum(1)
            with dve.Fori(0, UNITS - 2) as unit:
                for n in range(HPU * TT):
                    row_maximum(HPU * TT * (unit + 2) + n, n // TT, n % TT)
                split_maximum(unit + 2)
                normalise(unit)
            normalise(UNITS - 2)
            normalise(UNITS - 1)

            def low(b, buffer, hi_done, done):
                hi, lo, both = buffer
                dve.wait_ge(hi_done, 2 * b + 1)
                dve.tensor_tensor(lo[:, :], ps[:, 0, :], hi[:, :].bitcast(F32), ALU.subtract).then_inc(done, 1)
                dve.wait_ge(hi_done, 2 * b + 2)
                dve.tensor_tensor(both[CB:P, :], ps[CB:P, 1, :], both[CB:P, :].bitcast(F32),
                                  ALU.subtract).then_inc(done, 1)

            def residual_and_norm(b):
                for i in range(2):
                    rows = h[:, bass.ds(TT * b + 2 * i, 2), :]
                    dve.wait_ge(proj_mm, 2 * b + i + 1)
                    dve.tensor_tensor(rows, ps[:, 2 + i, :].rearrange("p (t c) -> p t c", t=2)[:, :, 0:C], rows,
                                      ALU.add).then_inc(h1_ready, 1)
                wait_apart(dve, h1_ready, 2 * b + 2)
                for t in range(TT):
                    dve.bn_stats(stats[:, t, :], h[:, bass.ds(TT * b + t, 1), :].rearrange("p o c -> p (o c)")).then_inc(stats2, 1)
                wait_apart(dve, stats2, TT * b + TT)
                for t in range(TT):
                    dve.bn_aggr(mv[:, t, :], stats[:, t, :]).then_inc(aggr2, 1)
                dve.wait_ge(rstd2, b + 1)
                for t in range(TT):
                    normal(z[:, 0, t, :], h[:, bass.ds(TT * b + t, 1), :].rearrange("p o c -> p (o c)"), t, z2_done)

            def split_hidden(b):
                for m in range(FT):
                    dve.wait_ge(gelu_done, FT * b + m + 1)
                    dve.tensor_copy(hid[0][:, m, :], hid32[:, m % 2, :]).then_inc(hid_hi, 1)
                    dve.wait_ge(hid_hi, FT * b + m + 1)
                    dve.tensor_tensor(hid[1][:, m, :], hid32[:, m % 2, :], hid[0][:, m, :].bitcast(F32),
                                      ALU.subtract).then_inc(hid_lo, 1)

            def result(b, i):
                rows = h[:, bass.ds(TT * b + 2 * i, 2), :]
                dve.wait_ge(f2_mm, 2 * b + i + 1)
                dve.tensor_tensor(rows, ps[:, 6 + i, :].rearrange("p (t c) -> p t c", t=2)[:, :, 0:C], rows,
                                  ALU.add).then_inc(y_ready, 1)

            dve.wait_ge(bias_added, 1)
            low(0, X[0], aT_hi, aT_lo)
            residual_and_norm(0)
            low(0, X[1], zT_hi, zT_lo)
            with dve.Fori(0, BATCH - 1) as b:
                low(b + 1, X[0], aT_hi, aT_lo)
                split_hidden(b)
                residual_and_norm(b + 1)
                result(b, 0)
                result(b, 1)
                low(b + 1, X[1], zT_hi, zT_lo)
            split_hidden(BATCH - 1)
            result(BATCH - 1, 0)
            result(BATCH - 1, 1)

        @block.tensor
        def _(pe):
            mm = pe.matmul

            pe.nop().then_inc(pv_done, KT)
            pe.nop().then_inc(o_turned, 1)
            pe.nop().then_inc(attn_ready, 1)
            pe.nop().then_inc(y_ready, 2)
            pe.nop().then_inc(hid_lo, 2)

            pe.wait_ge(consts, 4)
            for n, (_, _, tiles, _, _, _) in enumerate(weight_jobs):
                pe.wait_ge(doubled, (1, 1, 2, 3, 4, 4, 4, 4)[n])
                if n >= 4:
                    pe.wait_ge(w_lo_done, n - 3)
                for src, col in tiles:
                    rows = src.shape[0]
                    last = pe.transpose(ps[:, 4 + n % 4, col:col + rows], src, ident[0:rows, 0:rows])
                last.then_inc(turned, 1)
            for b in range(BATCH):
                pe.wait_ge(z_done, 2 * TT * (b + 1))
                for c in range(2):
                    k = 2 * b + c
                    if k >= 4:
                        pe.wait_ge(untied, k - 3)
                    for t in range(TT):
                        last = pe.transpose(ps[:, k % 4, t * P:(t + 1) * P],
                                            z[:, b % 2, t, c * P:(c + 1) * P], ident[:, :])
                    last.then_inc(turned, 1)

            def scores_for_max(b, g, head, chunk, tiles, first=False):
                if head == 0 and 0 in tiles:
                    pe.wait_ge(qk_in[g], Q_DMAS * (b + 1))
                for t in tiles:
                    if not (first and t < 2):
                        pe.wait_ge(a_read, TT * chunk + t - 1)
                    mm(ps[:, t % 2, :], QS[g][0:STACK, head, t * P:(t + 1) * P], KS[g][0:STACK, head, :],
                       start=True, stop=True).then_inc(a_mm, 1)

            def turn_max(unit):
                pe.wait_ge(m_parts, 4 * unit + 4)
                pe.wait_ge(attn_ready, 1 if isinstance(unit, int) and unit == 0 else unit)
                for t in range(TT):
                    last = pe.transpose(ps[0:PARTS * HPU, 7, :].bitcast(BF16)[:, t * P:(t + 1) * P],
                                        mparts[:, t, :, :].rearrange("p a h -> p (a h)"), ident16[:, :])
                last.then_inc(m_turned, 1)

            def scores(b, g, kt, step, pairs=range(PAIRS), first=False):
                if kt == 0 and 0 in pairs:
                    pe.wait_ge(m_in[g], M_DMAS * (b + 1))
                for pair in pairs:
                    if not first:
                        pe.wait_ge(p_ready, PAIRS * (step - 1) + pair + 1)
                    for head in (2 * pair, 2 * pair + 1):
                        last = mm(ps[:, 2 + head, :], KS[g][:, head, kt * P:(kt + 1) * P], QS[g][:, head, :],
                                  start=True, stop=True)
                    last.then_inc(b_mm, 1)

            def weigh(unit, g, kt, first=False):
                pe.wait_ge(p_ready, PAIRS * (KT * unit + kt + 1))
                if kt == 0:
                    pe.wait_ge(vu_ready, unit + 1)
                    pe.wait_ge(o_taken, unit)
                for head in range(HPU):
                    last = mm(ps[head * TILE_COLS:(head + 1) * TILE_COLS, 6, :], VU[g][:, kt, head, :],
                              prob[:, kt, head, :], start=kt == 0, stop=kt == KT - 1)
                last.then_inc(pv_done, 1)

            def turn_out(unit, final=False):
                pe.wait_ge(o_taken, unit + 1)
                pe.wait_ge(m_taken, unit + 2 - final)
                pe.wait_ge(attn_ready, 1 + unit)
                for t in range(TT):
                    last = pe.transpose(ps[:, 7, t * P:(t + 1) * P], o_sb[:, t * P:(t + 1) * P], ident[:, :])
                last.then_inc(o_turned, 1)

            def at(b, g, steps):
                return b + (g + steps) // GROUPS, (g + steps) % GROUPS

            def chunk(b, g, ahead, tiles=range(TT), first=False):
                nb, ng = at(b, g, ahead // HPU)
                if isinstance(nb, int) and nb >= BATCH:
                    return
                scores_for_max(nb, ng, ahead % HPU, HPU * (GROUPS * b + g) + ahead, tiles, first)

            def step(b, g, kt):
                unit = GROUPS * b + g
                nb, ng = at(b, g, (kt + 1) // KT)
                more = not (isinstance(nb, int) and nb == BATCH)
                for pair in range(PAIRS):
                    if more:
                        scores(nb, ng, (kt + 1) % KT, KT * unit + kt + 1, (pair,))
                    chunk(b, g, LEAD + kt, (pair,))
                if kt == 1 and not (isinstance(b, int) and unit == UNITS - 1):
                    turn_max(unit + 1)
                chunk(b, g, LEAD + kt, (2,))
                weigh(unit, g, kt)
                chunk(b, g, LEAD + kt, (3,))

            def unit_steps(b, g):
                unit = GROUPS * b + g
                final = isinstance(b, int) and unit == UNITS - 1
                for kt in range(1, KT):
                    step(b, g, kt)
                if not final:
                    nb, ng = at(b, g, 1)
                    step(nb, ng, 0)
                turn_out(unit, final)

            WX = ((0, 0, 0), (0, 0, 1), (1, 0, 0), (0, 1, 2), (1, 1, 2))

            pe.wait_ge(untied, 2 * BATCH)
            pe.wait_ge(w_lo_done, WJ)

            def early_banks(n, count):
                for i in range(n, n + count):
                    chunk(0, 0, i // TT, (i % TT,), first=i < TT)
                return n + count

            early, due = 0, 0
            for b in range(BATCH):
                for tile in range(QKT):
                    if b:
                        pe.wait_ge(hi_done, QKT * (b - 1) + tile + 1)
                    cols = slice(tile * P, (tile + 1) * P)
                    for i, (w, c, n) in enumerate(WX):
                        if tile == 0 and i in (0, 1, 3):
                            if b == 0:
                                pe.wait_ge(w_scaled, (1, 2, None, 4)[i])
                            pe.wait_ge(x_hi_done, 2 * b + 1) if i == 0 else pe.wait_ge(x_lo_done, 2 * b + (i + 1) // 2)
                        last = mm(ps[:, 2 + tile, :], qkvT[w][:, c, cols], X[b % 2][n][:, :],
                                  start=i == 0, stop=i == 4)
                    last.then_inc(qk_mm, 1)
                    early, due = early_banks(early, due), EARLY[b][tile]
                for t in range(TT):
                    n = TT * b + t
                    if n >= 3:
                        before = n - 3 if t >= 3 else TT * (b - 1) + (t if t else 3)
                        pe.wait_ge(v_taken, before + 1)
                    tok = slice(t * P, (t + 1) * P)
                    for i, (w, c, x_part) in enumerate(WX):
                        last = mm(ps[:, 5 + t % 3, 0:C], X[b % 2][x_part][:, tok], qkvT[w][:, c, 2 * C:3 * C],
                                  start=i == 0, stop=i == 4)
                    last.then_inc(v_mm, 1)
                    early, due = early_banks(early, due), EARLY[b][QKT + t]
            pe.wait_ge(v_taken, TT * (BATCH - 1) + 3)
            turn_max(0)
            early_banks(early, LEAD * TT - early)

            pe.wait_ge(hi_done, QKT * BATCH)
            pe.wait_ge(v_taken, TT * BATCH)
            pe.wait_ge(filled, 11)

            scores(0, 0, 0, 0, first=True)
            step(0, 0, 0)
            with pe.Fori(0, BATCH - 1) as b:
                for g in range(GROUPS):
                    unit_steps(b, g)
            for g in range(GROUPS):
                unit_steps(BATCH - 1, g)

            def turn(rows, done):
                for c in range(2):
                    for t in range(TT):
                        last = pe.transpose(ps[:, c, t * P:(t + 1) * P], rows[:, t, c * P:(c + 1) * P], ident[:, :])
                    last.then_inc(done, 1)

            def turn_attn(b):
                pe.wait_ge(a_copied, 2 * b + 2)
                if not (isinstance(b, int) and b == 0):
                    pe.wait_ge(zT_lo, 2 * b)
                turn(a_cur, a_turned)

            def turn_z(b):
                pe.wait_ge(z2_done, 2 * TT * (b + 1))
                turn(z[:, 0, :, :], z_turned)

            def project(b):
                pe.wait_ge(aT_lo, 2 * b + 2)
                for t in range(TT):
                    for i, (w, c, n) in enumerate(WX):
                        last = mm(ps[:, 2 + t // 2, (t % 2) * 256:(t % 2) * 256 + C],
                                  X[0][n][:, t * P:(t + 1) * P], projT[w][:, c, :], start=i == 0, stop=i == 4)
                    if t % 2:
                        last.then_inc(proj_mm, 1)

            def ffn1(b):
                pe.wait_ge(zT_lo, 2 * b + 2)
                for m in range(FT):
                    if m >= 2:
                        pe.wait_ge(gelu_done, FT * b + m - 1)
                    for i, (w, c, n) in enumerate(WX):
                        last = mm(ps[:, 4 + m % 2, :], w1T[w][:, c, m * P:(m + 1) * P], X[1][n][:, :],
                                  start=i == 0, stop=i == 4)
                    last.then_inc(f1_mm, 1)

            def ffn2(b):
                pe.wait_ge(hid_lo, 2 + FT * (b + 1))
                pe.wait_ge(y_ready, 2 + 2 * b)
                for t in range(TT):
                    for w, n in ((0, 0), (0, 1), (1, 0)):
                        for m in range(FT):
                            last = mm(ps[:, 6 + t // 2, (t % 2) * 256:(t % 2) * 256 + C],
                                      hid[n][:, m, t * P:(t + 1) * P], w2s[w][:, m, :],
                                      start=m + n + w == 0, stop=m == FT - 1 and w == 1)
                    if t % 2:
                        last.then_inc(f2_mm, 1)

            pe.wait_ge(w2_lo_done, 1)
            turn_attn(0)
            project(0)
            turn_z(0)
            with pe.Fori(0, BATCH - 1) as b:
                turn_attn(b + 1)
                ffn1(b)
                project(b + 1)
                ffn2(b)
                turn_z(b + 1)
            ffn1(BATCH - 1)
            ffn2(BATCH - 1)


_INS = ['x', 'L0_tok_weight', 'L0_attn_qkv_weight', 'L0_attn_qkv_bias', 'L0_attn_proj_weight', 'L0_attn_proj_bias',
        'L0_ffn_in_weight', 'L0_ffn_in_bias', 'L0_ffn_out_weight']


def kernel(**inputs):
    import numpy as _np
    import concourse.bacc as _bacc
    from concourse import mybir as _mybir
    from concourse.bass_utils import run_bass_kernel_spmd as _run

    nc = _bacc.Bacc("TRN2", target_bir_lowering=False, num_devices=1)
    arrays, args = {}, []
    for name in _INS:
        a = _np.ascontiguousarray(inputs[name])
        arrays[f"in_{name}_dram"] = a
        args.append(nc.dram_tensor(f"in_{name}_dram", a.shape, _mybir.dt.from_np(a.dtype), kind="ExternalInput").ap())
    shape = (*inputs['x'].shape, inputs['L0_tok_weight'].shape[1])
    args.append(nc.dram_tensor("out_0_dram", shape, _mybir.dt.float32, kind="ExternalOutput").ap())
    decoder_layer(nc, *args)
    r = _run(nc, [arrays], core_ids=[0])
    return r.results[0]["out_0_dram"]
```

```python
from contextlib import ExitStack

import concourse.bass as bass
from concourse import mybir

F32 = mybir.dt.float32
F32R = mybir.dt.float32r
BF16 = mybir.dt.bfloat16
I32 = mybir.dt.int32
U32 = mybir.dt.uint32
ALU = mybir.AluOpType
ACT = mybir.ActivationFunctionType
AX = mybir.AxisListType

P = 128
HEADS = 12
ALPHA = 0.35
EPS = 1e-5
FOUR_THIRDS_DOWN = 1.3333332538604736
EXPONENT_BITS = 0x7F800000
HPU = 4
TILE_COLS = 32
PARTS = 3
PRODUCTS = 7
Q_PART = (0, 0, 0, 1, 1, 1, 2)
K_PART = (0, 1, 2, 0, 1, 2, 0)
Q_RUNS = ((0, 3, 0, 0), (3, 3, 1, 0), (6, 1, 2, 0))
K_RUNS = ((0, 3, 0, 1), (3, 3, 0, 1), (6, 1, 0, 0))
LEAD = 7


def decoder_layer(nc, x, emb, qkv_w, qkv_b, proj_w, proj_b, ffn_w1, ffn_b1, ffn_w2, out):
    BATCH, SEQ = x.shape
    C = emb.shape[1]
    F = ffn_w1.shape[0]
    HD = C // HEADS
    SCALE = float(HD) ** -0.5
    CH = C // 2
    CB = C - P
    WIDE = P + 2 * CB
    TT = SEQ // P
    NT = BATCH * TT
    GROUPS = HEADS // HPU
    STACK = PRODUCTS * HD
    ROWS = STACK + PARTS
    KT = TT
    FT = F // P
    UNIT_CH = HPU * HD
    UNITS = BATCH * GROUPS

    BLOCKS = (((0, 0), (0, 1)), ((1, 0), (1, 1)), ((0, 2), (1, 2)))
    QKT = len(BLOCKS)
    qk_parts = nc.dram_tensor("qk_parts", [BATCH, QKT, PARTS, P, SEQ], BF16, kind="Internal").ap()
    out_t = out.rearrange("b (p t) c -> b p t c", p=P)

    with ExitStack() as ctx:
        def sb(name, shape, dt=F32):
            return ctx.enter_context(nc.sbuf_tensor(name, shape, dt))

        def sem(name):
            return ctx.enter_context(nc.semaphore(name))

        ps = ctx.enter_context(nc.psum_tensor("ps", [P, 8, 512], F32))

        ids = sb("ids", [P, NT], I32)
        h = sb("h", [P, NT, C])
        z = sb("z", [P, 2, TT, WIDE])
        stats = sb("stats", [P, NT, 6])
        mv = sb("mv", [P, NT, 2])
        rstd = sb("rstd", [P, NT])
        minus_half = sb("minus_half", [P, TT])
        eps = sb("eps", [P, 1])
        root = sb("root", [P, NT])
        table = sb("table", [P, 1])
        ident = sb("ident", [P, P])
        ident16 = sb("ident16", [P, P], BF16)

        prob = sb("prob", [P, KT, HPU, SEQ])

        def borrow(kt, at, *shape):
            room = prob[:, kt:kt + 2, :, :].rearrange("p k h n -> p (k h n)")
            return room[:, at:at + shape[0] * shape[1]].rearrange("p (a b) -> p a b", a=shape[0])

        wq_nat = borrow(0, 0, QKT, WIDE)
        w1_nat = borrow(0, QKT * WIDE, FT, WIDE)
        wv_nat = borrow(0, (QKT + FT) * WIDE, 2, WIDE)[0:CH]
        wp_nat = borrow(0, (QKT + FT + 2) * WIDE, 2, WIDE)[0:CH]
        qk32, rest = borrow(2, 0, QKT, SEQ), borrow(2, QKT * SEQ, QKT, SEQ)
        qkvT = [sb(f"qkvT_{n}", [P, 2, 3 * C], F32R) for n in ("hi", "lo")]
        projT = [sb(f"projT_{n}", [P, 2, C], F32R) for n in ("hi", "lo")]
        w1T = [sb(f"w1T_{n}", [P, 2, F], F32R) for n in ("hi", "lo")]
        w2 = sb("w2", [P, FT, C])
        w2s = [sb(f"w2_{n}", [P, FT, C], F32R) for n in ("hi", "lo")]
        vbias = sb("vbias", [P, C])
        pbias = sb("pbias", [P, C])
        X = [[sb(f"X{i}_{n}", [P, SEQ], F32R) for n in ("hi", "lo", "both")] for i in range(2)]
        b1 = sb("b1", [P, FT])
        qkb = sb("qkb", [P, QKT])
        qkb_s = sb("qkb_s", [P, QKT])
        qk_scale = sb("qk_scale", [P, QKT])

        xT = sb("xT", [P, 2, BATCH * SEQ])
        attn = xT[:, :, :].rearrange("p a (b c) -> p (a b) c", c=UNIT_CH)[:, 0:UNITS * TT, :].rearrange(
            "p (u t) c -> p u t c", u=UNITS)
        xmax_b = sb("xmax_b", [P, 2, BATCH])
        xmax = sb("xmax", [P, 2])
        wmax_p = sb("wmax_p", [P, 2, 2])
        wmax = sb("wmax", [P, 2])
        powers = sb("powers", [P, 2, 2])
        xpow = sb("xpow", [P, 2])
        wpow = sb("wpow", [P, 2])
        raw = sb("raw", [P, 2])
        raw43 = sb("raw43", [P, 2])
        cs = sb("cs", [P, 2])
        inv = sb("inv", [P, 2])

        parts = sb("parts", [P, 2, QKT, PARTS, SEQ], BF16)
        room = parts[:, :, :, :, :].rearrange("p a b c n -> p (a b c n)").bitcast(F32)
        a_cur = room[:, 0:TT * WIDE].rearrange("p (t c) -> p t c", t=TT)
        hid32 = room[:, TT * WIDE:TT * WIDE + FT * SEQ].rearrange("p (m n) -> p m n", m=FT)
        v_all = sb("v_all", [P, BATCH, KT, C])

        QS = [sb(f"QS{g}", [ROWS, HPU, SEQ], BF16) for g in range(GROUPS)]
        KS = [sb(f"KS{g}", [ROWS, HPU, SEQ], BF16) for g in range(GROUPS)]
        VU = [sb(f"VU{g}", [P, KT, HPU, TILE_COLS]) for g in range(GROUPS)]
        negmax = sb("negmax", [P, UNITS, TT, HPU])
        negrest = sb("negrest", [P, TT, HPU])
        mparts = sb("mparts", [P, TT, PARTS, HPU], BF16)
        mrows = sb("mrows", [PARTS * HPU, SEQ], BF16)
        ones = mrows[0:PARTS, :]
        o_sb = z[:, 1, 0:2, :].rearrange("p t c -> p (t c)")
        rden = sb("rden", [P, TT, HPU])

        hid = [sb(f"hid_{n}", [P, FT, SEQ], F32R) for n in ("hi", "lo")]
        newton = sb("newton", [P, 2, NT])

        ids_in = sem("ids_in")
        gathered = [sem(f"gathered{b}") for b in range(BATCH)]
        wq_in, wp_in, w1_in, small_in, w2_in = (sem(n) for n in ("wq_in", "wp_in", "w1_in", "small_in", "w2_in"))
        consts = sem("consts")
        stats_done, aggr_done, rstd_steps, z_done = (sem(n) for n in ("stats_done", "aggr_done", "rstd_steps", "z_done"))
        root_done, wv_in = sem("root_done"), sem("wv_in")
        bias_added = sem("bias_added")
        wmax_steps, w2_hi_done, w2_lo_done, doubled = (sem(n) for n in ("wmax_steps", "w2_hi_done", "w2_lo_done", "doubled"))
        turned, untied = sem("turned"), sem("untied")
        w_turned, w_raw_done, w_hi_done, w_lo_done = (sem(n) for n in ("w_turned", "w_raw_done", "w_hi_done", "w_lo_done"))
        z_twice, z2_twice = sem("z_twice"), sem("z2_twice")
        table_loads = sem("table_loads")
        ones_in, far_scaled = sem("ones_in"), sem("far_scaled")
        xmax_steps, xmax_ready, wmax_ready = (sem(n) for n in ("xmax_steps", "xmax_ready", "wmax_ready"))
        xpow_ready, wpow_ready, cs_steps, w_scaled = (sem(n) for n in ("xpow_ready", "wpow_ready", "cs_steps", "w_scaled"))
        filled = sem("filled")
        qkb_ready = sem("qkb_ready")
        x_hi_done, x_lo_done, qk_mm, qk_taken, v_mm, v_taken = (sem(n) for n in ("x_hi_done", "x_lo_done", "qk_mm", "qk_taken", "v_mm", "v_taken"))
        hi_done, rest_done, mid_done, lo_done = (sem(n) for n in ("hi_done", "rest_done", "mid_done", "lo_done"))
        stored = [[sem(f"stored{i}_{j}") for j in range(QKT)] for i in range(2)]
        qk_in = [sem(f"qk_in{g}") for g in range(GROUPS)]
        m_in = [sem(f"m_in{g}") for g in range(GROUPS)]
        vu_ready = sem("vu_ready")
        a_mm, a_read = sem("a_mm"), sem("a_read")
        m_parts, m_turned, m_taken = (sem(n) for n in ("m_parts", "m_turned", "m_taken"))
        b_mm, p_ready = sem("b_mm"), sem("p_ready")
        pv_done = sem("pv_done")
        o_taken, o_turned, rden_ready, attn_ready = (sem(n) for n in ("o_taken", "o_turned", "rden_ready", "attn_ready"))
        act_hi = sem("act_hi")
        a_copied, a_turned, aT_hi, aT_lo, proj_mm, h1_ready = (sem(n) for n in ("a_copied", "a_turned", "aT_hi", "aT_lo", "proj_mm", "h1_ready"))
        stats2, aggr2, eps2, rstd2, z2_done, z_turned, zT_hi, zT_lo = (sem(n) for n in ("stats2", "aggr2", "eps2", "rstd2", "z2_done", "z_turned", "zT_hi", "zT_lo"))
        f1_mm, gelu_done, hid_hi, hid_lo, f2_mm, y_ready, y_out = (sem(n) for n in ("f1_mm", "gelu_done", "hid_hi", "hid_lo", "f2_mm", "y_ready", "y_out"))


        def nat(tile, rows, j, c):
            return tile[0:rows, j, c * P:(c + 1) * P]

        weight_jobs = [(wq_in, 96, [(nat(wq_nat, P, j, c), j * P) for j in range(QKT)], qkvT, c, 0) for c in range(2)]
        weight_jobs += [(wv_in, 16, [(nat(wv_nat, CH, j, c), c * C + j * CH) for c in range(2) for j in range(2)],
                         qkvT, None, 2 * C)]
        weight_jobs += [(wp_in, 16, [(nat(wp_nat, CH, j, c), c * C + j * CH) for c in range(2) for j in range(2)],
                         projT, None, 0)]
        weight_jobs += [(w1_in, 16, [(nat(w1_nat, P, 3 * k + j, c), j * P) for j in range(3)], w1T, c, 3 * k * P)
                        for c in range(2) for k in range(2)]
        JOB_COLS = 3 * P

        def job_views(n):
            _, _, _, dst, c, col = weight_jobs[n]
            bank = ps[:, 4 + n % 4, 0:JOB_COLS]
            if c is None:
                return (bank.rearrange("p (c n) -> p c n", c=2), *(d[:, :, col:col + C] for d in dst))
            return (bank, *(d[:, c, col:col + JOB_COLS] for d in dst))

        WJ = len(weight_jobs)
        WEIGHTS_AFTER = ((), (4, 5), (6, 7), ())
        QKV_JOBS = 3

        def raw_weights(n):
            room = v_all[:, :, :, :].rearrange("p b t c -> p (b t c)")
            end = BATCH * KT * C - (WJ - 1 - n) * JOB_COLS
            tile = room[:, end - JOB_COLS:end]
            return tile.rearrange("p (c n) -> p c n", c=2) if weight_jobs[n][4] is None else tile

        FILLED = 5 + 2 * QKT + 2 * GROUPS
        LAST = KT * UNITS - 1
        BY_ACT = (1, 3)
        BY_DVE = tuple(m for m in range(FT) if m not in BY_ACT)
        PAIRS = HPU // 2
        Q_DMAS = 16 * (len(Q_RUNS) + len(K_RUNS))
        M_DMAS = 16
        MAX_AFTER = 1
        BEFORE_SCORES = 24
        EARLY = ((0,) * (QKT + TT), (0,) * (QKT + TT), (0, 0, 2, 2, 2, 2, 2), (3, 3, 3, 1, 1, 1, 1))

        UNIT_BANKS = HPU * TT
        MAX_SLOT = 2

        def max_bank(j, early):
            return j % 2 if early else (0, 1, 7)[(j + (j >= MAX_SLOT)) % 3]

        def turned_max_bank(unit):
            return 2 if isinstance(unit, int) and unit == 0 else 7

        def wait_apart(engine, semaphore, value):
            engine.wait_ge(semaphore, value)
            engine.sem_inc(passed, 1)

        passed = sem("passed")
        block = ctx.enter_context(nc.Block())

        @block.sync
        def _(sp):
            sp.dma_start(ids[:, :].rearrange("p (b t) -> p b t", t=TT), x.rearrange("b (p t) -> p b t", t=TT)).then_inc(ids_in, 16)
            for tile, halves in enumerate(BLOCKS):
                for half, (side, g) in enumerate(halves):
                    row = side * C + g * UNIT_CH
                    sp.dma_start(wq_nat[half * UNIT_CH:(half + 1) * UNIT_CH, tile, 0:C],
                                 qkv_w[row:row + UNIT_CH, :].rearrange("(h d) c -> d h c", d=HD)).then_inc(wq_in, 16)
            sp.dma_start(wv_nat[:, :, 0:C], qkv_w[2 * C:3 * C, :].rearrange("(j p) c -> p j c", p=CH)).then_inc(wv_in, 16)
            sp.dma_start(wp_nat[:, :, 0:C], proj_w.rearrange("(j p) c -> p j c", p=CH)).then_inc(wp_in, 16)
            sp.dma_start(w1_nat[:, :, 0:C], ffn_w1.rearrange("(j p) c -> p j c", p=P)).then_inc(w1_in, 16)
            for tile, halves in enumerate(BLOCKS):
                for half, (side, g) in enumerate(halves):
                    row = side * C + g * UNIT_CH
                    sp.dma_start(qkb[half * UNIT_CH:(half + 1) * UNIT_CH, tile:tile + 1],
                                 qkv_b[row:row + UNIT_CH].rearrange("(h d o) -> d h o", d=HD, o=1),
                                 allow_slow_non_contiguous=True).then_inc(small_in, 16)
            sp.dma_start(vbias[:, :], qkv_b[2 * C:3 * C].rearrange("(a c) -> a c", a=1).broadcast_to([P, C])).then_inc(small_in, 16)
            sp.dma_start(pbias[:, :], proj_b.rearrange("(a c) -> a c", a=1).broadcast_to([P, C])).then_inc(small_in, 16)
            sp.dma_start(b1[:, :], ffn_b1.rearrange("(j p) -> p j", p=P), allow_slow_non_contiguous=True).then_inc(small_in, 16)
            sp.dma_start(w2[:, :, :], ffn_w2.rearrange("(j p) c -> p j c", p=P)).then_inc(w2_in, 16)
            sp.wait_ge(filled, 5)
            for g in range(GROUPS):
                sp.dma_start(KS[g][STACK:ROWS, :, :], ones[:, :].unsqueeze(1).broadcast_to([PARTS, HPU, SEQ])).then_inc(ones_in, 16)

            def store_parts(b, tiles=range(QKT)):
                for tile in tiles:
                    sp.wait_ge(lo_done, QKT * b + tile + 1)
                    sp.dma_start(qk_parts[b, tile].rearrange("n r s -> r n s"), parts[:, b % 2, tile, :, :]).then_inc(stored[b % 2][tile], 16)

            def load_unit(b, g):
                for to, side, (n, count, first, step) in [(QS[g], 0, run) for run in Q_RUNS] + [(KS[g], 1, run) for run in K_RUNS]:
                    tile, half = next((i, j) for i in range(QKT) for j in range(2) if BLOCKS[i][j] == (side, g))
                    rows = slice(half * UNIT_CH, (half + 1) * UNIT_CH)
                    last = first + (count if step else 1)
                    piece = qk_parts[bass.ds(b, 1), tile, first:last, rows, :].rearrange(
                        "o n (d h) s -> (o n) d (h s)", d=HD).broadcast_to([count, HD, HPU * SEQ])
                    sp.dma_start(to[n * HD:(n + count) * HD, :, :].rearrange("r h s -> r (h s)"), piece).then_inc(qk_in[g], 16)

            store_parts(0, (0, 1))
            sp.wait_ge(stored[0][0], 16)
            sp.wait_ge(stored[0][1], 16)
            load_unit(0, 0)
            store_parts(0, (2,))
            store_parts(1)
            load_unit(0, 1)
            store_parts(2)
            sp.wait_ge(stored[0][2], 16)
            load_unit(0, 2)
            store_parts(3)
            for tile in range(QKT):
                for buffer in stored:
                    sp.wait_ge(buffer[tile], 16 * BATCH // 2)
            with sp.Fori(1, BATCH) as b:
                for g in range(GROUPS):
                    sp.wait_ge(b_mm, PAIRS * KT * (GROUPS * (b - 1) + g + 1))
                    load_unit(b, g)

            with sp.Fori(0, BATCH) as b:
                sp.wait_ge(y_ready, 2 + 2 * b + 2)
                sp.dma_start(out_t[bass.ds(b, 1), :, :, :].rearrange("o p t c -> p (o t) c"),
                             h[:, bass.ds(TT * b, TT), :]).then_inc(y_out, 16)
            sp.wait_ge(y_out, 16 * BATCH)

        @block.gpsimd
        def _(gp):
            gp.wait_ge(ids_in, 16)

            def gather(b):
                for t in range(b * TT, (b + 1) * TT):
                    gp.indirect_dma_start(
                        out=h[:, t, :], out_offset=None, in_=emb[:, :],
                        in_offset=bass.IndirectOffsetOnAxis(ap=ids[:, t:t + 1], axis=0),
                    ).then_inc(gathered[b], 16)

            gather(0)
            gp.memset(ident[:, :], 0.0).then_inc(consts, 1)
            gp.memset(ident16[:, :], 0.0).then_inc(consts, 1)
            gp.wait_ge(consts, 2)
            for m in (ident, ident16):
                gp.affine_select(out=m[:, :], in_=m[:, :], compare_op=ALU.not_equal, fill=1.0,
                                 base=0, pattern=[[-1, P]], channel_multiplier=1).then_inc(consts, 1)
            gather(1)
            gather(2)
            gather(3)
            for n in range(WJ):
                _, hi, lo = job_views(n)
                gp.wait_ge(w_raw_done, n + 1)
                gp.wait_ge(w_hi_done, n + 1)
                gp.tensor_tensor(lo, raw_weights(n), hi.bitcast(F32), ALU.subtract).then_inc(w_lo_done, 1)
            gp.wait_ge(wmax_ready, 1)
            gp.wait_ge(filled, 4)
            gp.tensor_tensor(wpow[:, :], wmax[:, :], powers[:, 1, :], ALU.pow).then_inc(wpow_ready, 1)
            gp.wait_ge(xmax_ready, 1)
            gp.tensor_tensor(xpow[:, :], xmax[:, :], powers[:, 0, :], ALU.pow).then_inc(xpow_ready, 1)

            def split_maximum(unit):
                minus = negmax[:, bass.ds(unit, 1), :, :].rearrange("p o t h -> p (o t) h")
                if not (isinstance(unit, int) and unit == 0):
                    gp.wait_ge(m_turned, unit)
                wait_apart(gp, a_read, UNIT_BANKS * (unit + 1))
                gp.tensor_copy(mparts[:, :, 0, :], minus).then_inc(m_parts, 1)
                wait_apart(gp, m_parts, 4 * unit + 1)
                gp.tensor_tensor(negrest[:, :, :], minus, mparts[:, :, 0, :], ALU.subtract).then_inc(m_parts, 1)
                wait_apart(gp, m_parts, 4 * unit + 2)
                gp.tensor_copy(mparts[:, :, 1, :], negrest[:, :, :]).then_inc(m_parts, 1)
                gp.wait_ge(m_parts, 4 * unit + 3)
                gp.tensor_tensor(mparts[:, :, 2, :], negrest[:, :, :], mparts[:, :, 1, :], ALU.subtract).then_inc(m_parts, 1)

            for n in range(QKT * BATCH):
                b, tile = n // QKT, n % QKT
                if n == QKT * BATCH - 1:
                    split_maximum(0)
                gp.wait_ge(mid_done, n + 1)
                gp.tensor_tensor(parts[:, b % 2, tile, 2, :], rest[:, tile, :], parts[:, b % 2, tile, 1, :], ALU.subtract).then_inc(lo_done, 1)

            def copy_v(b, g):
                chs = slice(g * UNIT_CH, (g + 1) * UNIT_CH)
                gp.tensor_tensor(
                    VU[g][:, :, :, 0:HD],
                    v_all[:, bass.ds(b, 1), :, chs].rearrange("p o t (h c) -> p (o t) h c", c=HD),
                    vbias[:, chs].rearrange("p (h c) -> p h c", c=HD).unsqueeze(1).broadcast_to([P, KT, HPU, HD]),
                    ALU.add).then_inc(vu_ready, 1)

            gp.wait_ge(v_taken, TT * BATCH)
            gp.wait_ge(filled, FILLED)
            for g in range(GROUPS):
                copy_v(0, g)
            gp.wait_ge(z_done, NT)
            gp.tensor_tensor(h[:, :, :], h[:, :, :], pbias[:, :].unsqueeze(1).broadcast_to([P, NT, C]),
                             ALU.add).then_inc(bias_added, 1)
            split_maximum(1)
            gp.wait_ge(w2_in, 16)
            gp.tensor_copy(w2s[0][:, :, :], w2[:, :, :]).then_inc(w2_hi_done, 1)
            gp.wait_ge(w2_hi_done, 1)
            gp.tensor_tensor(w2s[1][:, :, :], w2[:, :, :], w2s[0][:, :, :].bitcast(F32), ALU.subtract).then_inc(w2_lo_done, 1)
            with gp.Fori(1, BATCH) as b:
                for g in range(GROUPS):
                    split_maximum(GROUPS * (b - 1) + g + 2)
                    gp.wait_ge(pv_done, KT + KT * (GROUPS * (b - 1) + g + 1))
                    copy_v(b, g)

            def rstd_of(b):
                wait_apart(gp, aggr2, TT * b + TT)
                gp.tensor_scalar(rstd[:, 0:TT], mv[:, 0:TT, 1], EPS, None, ALU.add).then_inc(eps2, 1)
                gp.wait_ge(eps2, b + 1)
                gp.tensor_tensor(rstd[:, 0:TT], rstd[:, 0:TT], minus_half[:, 0:TT], ALU.pow).then_inc(rstd2, 1)

            def copy_attn(b):
                gp.wait_ge(attn_ready, 1 + GROUPS * (b + 1))
                if not (isinstance(b, int) and b == 0):
                    gp.wait_ge(a_turned, 2 * b)
                rows = attn[:, bass.ds(GROUPS * b, GROUPS), :, :].rearrange("p g t c -> p t g c")
                gp.tensor_copy(a_cur[:, :, 0:P].rearrange("p t (g c) -> p t g c", g=2),
                               rows[:, :, 0:2, :]).then_inc(a_copied, 1)
                gp.tensor_copy(a_cur[:, :, P:WIDE].rearrange("p t (g c) -> p t g c", g=2),
                               rows[:, :, 2:3, :].broadcast_to([P, TT, 2, CB])).then_inc(a_copied, 1)

            def twice(b):
                wait_apart(gp, z2_done, TT * (b + 1))
                gp.tensor_copy(z[:, 0, :, C:WIDE], z[:, 0, :, P:C]).then_inc(z2_twice, 1)

            copy_attn(0)
            split_maximum(UNITS - 1)
            rstd_of(0)
            twice(0)
            copy_attn(1)
            with gp.Fori(1, BATCH - 1) as b:
                copy_attn(b + 1)
                rstd_of(b)
                twice(b)
            rstd_of(BATCH - 1)
            twice(BATCH - 1)

        @block.scalar
        def _(act):
            def roots(b):
                here = slice(b * TT, (b + 1) * TT)
                act.wait_ge(aggr_done, TT * (b + 1))
                act.activation(root[:, here], mv[:, here, 1], ACT.Sqrt, bias=eps[:, 0:1]).then_inc(root_done, 1)

            def high_weights(jobs):
                for n in jobs:
                    bank, hi, _ = job_views(n)
                    act.wait_ge(w_turned, n + 1)
                    act.activation(raw_weights(n), bank, ACT.Copy).then_inc(w_raw_done, 1)
                    act.activation(hi, bank, ACT.Copy).then_inc(w_hi_done, 1)

            def twice(b):
                act.wait_ge(z_done, TT * (b + 1))
                act.activation(z[:, b % 2, :, C:WIDE], z[:, b % 2, :, P:C], ACT.Copy).then_inc(z_twice, 1)

            act.wait_ge(filled, 1)
            act.activation(table[:, :], eps[:, :], ACT.Sqrt).then_inc(table_loads, 1)
            for tile, loaded, count in ((wq_nat, wq_in, 96), (wv_nat, wv_in, 16), (wp_nat, wp_in, 16), (w1_nat, w1_in, 16)):
                act.wait_ge(loaded, count)
                act.activation(tile[:, :, C:WIDE], tile[:, :, P:C], ACT.Copy).then_inc(doubled, 1)
            high_weights(range(2))
            roots(0)
            high_weights(range(2, 3))
            for b in range(BATCH):
                twice(b)
                if b == 0:
                    high_weights(range(3, 4))
                if b + 1 < BATCH:
                    roots(b + 1)
                for k in (2 * b, 2 * b + 1):
                    act.wait_ge(turned, k + 1)
                    act.activation(xT[:, k % 2, b * SEQ:(b + 1) * SEQ], ps[:, k % 4, :], ACT.Copy).then_inc(untied, 1)
                high_weights(WEIGHTS_AFTER[b])

            act.wait_ge(qkb_ready, 1)
            act.wait_ge(filled, 5 + 2 * QKT)

            def smooth_hi(b):
                if b >= 2:
                    act.wait_ge(v_mm, TT * (b - 1))
                for c, to in ((0, X[b % 2][0]), (1, X[b % 2][2])):
                    act.activation(to[:, :], xT[:, c, b * SEQ:(b + 1) * SEQ], ACT.Copy,
                                   scale=inv[:, c:c + 1]).then_inc(x_hi_done, 1)

            def max_rows(b, g, first=False):
                act.wait_ge(m_turned, GROUPS * b + g + 1)
                if first:
                    act.wait_ge(ones_in, 16 * GROUPS)
                else:
                    before = (b, g - 1) if g else (b - 1, GROUPS - 1)
                    act.wait_ge(m_in[before[1]], M_DMAS * (before[0] + 1))
                act.activation(mrows[:, :], ps[0:PARTS * HPU, turned_max_bank(GROUPS * b + g), :].bitcast(BF16)[:, 0:SEQ],
                               ACT.Copy).then_inc(m_taken, 1)
                act.wait_ge(m_taken, GROUPS * b + g + 1)
                act.dma_start(QS[g][STACK:ROWS, :, :], mrows[:, :]).then_inc(m_in[g], 16)

            def qkv_out(b, first=False):
                for tile in range(QKT):
                    act.wait_ge(qk_mm, QKT * b + tile + 1)
                    if not first:
                        act.wait_ge(lo_done, QKT * (b - 1) + tile + 1)
                    if b >= 2:
                        act.wait_ge(stored[b % 2][tile], 16 * (b // 2))
                    act.activation(qk32[:, tile, :], ps[:, 2 + tile, :], ACT.Identity, bias=qkb_s[:, tile:tile + 1],
                                   scale=qk_scale[:, tile:tile + 1]).then_inc(qk_taken, 1)
                    act.activation(parts[:, b % 2, tile, 0, :], ps[:, 2 + tile, :], ACT.Identity, bias=qkb_s[:, tile:tile + 1],
                                   scale=qk_scale[:, tile:tile + 1]).then_inc(hi_done, 1)
                for t in range(TT):
                    act.wait_ge(v_mm, TT * b + t + 1)
                    act.activation(v_all[:, b, t, :], ps[:, 5 + t % 3, 0:C], ACT.Copy).then_inc(v_taken, 1)
                    if b == BATCH - 1 and t == MAX_AFTER:
                        max_rows(0, 0, first=True)

            act.wait_ge(cs_steps, 5)
            smooth_hi(0)
            act.wait_ge(w_lo_done, QKV_JOBS)
            for part in qkvT:
                act.activation(part[:, 1, :], part[:, 1, :].bitcast(F32), ACT.Copy, scale=cs[:, 1:2]).then_inc(far_scaled, 1)
            for b in range(BATCH):
                if b + 1 < BATCH:
                    smooth_hi(b + 1)
                qkv_out(b, first=b == 0)

            def exps(step, kt):
                for pair in range(PAIRS):
                    act.wait_ge(b_mm, PAIRS * step + pair + 1)
                    if pair == 0:
                        act.wait_ge(pv_done, step + 1)
                    act.activation(prob[:, kt, 2 * pair:2 * pair + 2, :],
                                   ps[:, 2 + 2 * pair:4 + 2 * pair, :], ACT.Exp).then_inc(p_ready, 1)

            def out_copy(unit):
                act.wait_ge(pv_done, KT + KT * (unit + 1))
                act.wait_ge(o_turned, 1 + unit)
                act.activation(o_sb[:, :], ps[:, 6, :], ACT.Copy).then_inc(o_taken, 1)

            exps(0, 0)

            def unit_exps(b, g, last=False):
                unit = GROUPS * b + g
                exps(KT * unit + 1, 1)
                exps(KT * unit + 2, 2)
                if not last:
                    nb, ng = (b, g + 1) if g + 1 < GROUPS else (b + 1, 0)
                    max_rows(nb, ng)
                exps(KT * unit + 3, 3)
                if not last:
                    exps(KT * unit + 4, 0)
                out_copy(unit)

            with act.Fori(0, BATCH - 1) as b:
                for g in range(GROUPS):
                    unit_exps(b, g)
            for g in range(GROUPS):
                unit_exps(BATCH - 1, g, last=g == GROUPS - 1)

            def high(b, buffer, bank, ready, done):
                for c, to in ((0, buffer[0]), (1, buffer[2])):
                    act.wait_ge(ready, 2 * b + c + 1)
                    act.activation(to[:, :], ps[:, bank + c, :], ACT.Copy).then_inc(done, 1)

            def gelus(b):
                act.wait_ge(y_ready, 2 + 2 * b)
                for m in range(FT):
                    act.wait_ge(f1_mm, FT * b + m + 1)
                    act.wait_ge(hid_lo, FT * b + m + 1)
                    act.activation(hid32[:, m, :], ps[:, 4 + m % 2, :], ACT.Gelu, bias=b1[:, m:m + 1]).then_inc(gelu_done, 1)
                    if m in BY_ACT:
                        act.wait_ge(gelu_done, FT * b + m + 1)
                        act.activation(hid[0][:, m, :], hid32[:, m, :], ACT.Copy).then_inc(act_hi, 1)

            act.wait_ge(table_loads, 1)
            act.activation(table[:, :], eps[:, :], ACT.Gelu).then_inc(table_loads, 1)
            with act.Fori(0, BATCH - 2) as b:
                gelus(b)
                high(b + 1, X[1], 0, z_turned, zT_hi)
                high(b + 2, X[0], 2, a_turned, aT_hi)
            gelus(BATCH - 2)
            high(BATCH - 1, X[1], 0, z_turned, zT_hi)
            gelus(BATCH - 1)

        @block.vector
        def _(dve):
            dve.memset(eps[:, :], EPS).then_inc(filled, 1)
            dve.memset(minus_half[:, :], -0.5).then_inc(filled, 1)
            dve.memset(powers[:, 0, :], ALPHA).then_inc(filled, 1)
            dve.memset(powers[:, 1, :], ALPHA - 1.0).then_inc(filled, 1)
            dve.memset(ones[:, :], 1.0).then_inc(filled, 1)
            for tile, halves in enumerate(BLOCKS):
                for half, (side, _) in enumerate(halves):
                    dve.memset(qk_scale[half * UNIT_CH:(half + 1) * UNIT_CH, tile:tile + 1],
                               1.0 if side else SCALE).then_inc(filled, 1)
            for g in range(GROUPS):
                dve.memset(VU[g][:, :, :, HD:TILE_COLS], 0.0).then_inc(filled, 1)
            dve.wait_ge(filled, FILLED - GROUPS)
            for g in range(GROUPS):
                dve.memset(VU[g][:, :, :, HD:HD + 1], 1.0).then_inc(filled, 1)

            def normal(to, rows, t, done):
                dve.tensor_scalar(to[:, 0:C], rows, mv[:, t, 0:1], rstd[:, t:t + 1], ALU.subtract, ALU.mult).then_inc(done, 1)

            def largest_weight(n):
                dve.wait_ge(w_raw_done, n + 1)
                to = wmax_p[:, 0, n:n + 1] if n < 2 else wmax_p[:, 1, :]
                dve.tensor_reduce(to, raw_weights(n), AX.X, ALU.max, apply_absolute_value=True).then_inc(wmax_steps, 1)

            def row_stats(b, t):
                if t == 0:
                    dve.wait_ge(gathered[b], 16 * TT)
                dve.bn_stats(stats[:, b * TT + t, :], h[:, b * TT + t, :]).then_inc(stats_done, 1)

            def meanwhile(b, step):
                if b == 0 and step < QKV_JOBS:
                    largest_weight(step)
                if b in (1, 2) and step < TT:
                    row_stats(b + 1, step)

            def largest(b):
                dve.wait_ge(untied, 2 * (b + 1))
                dve.tensor_reduce(xmax_b[:, :, b], xT[:, :, b * SEQ:(b + 1) * SEQ], AX.X, ALU.max,
                                  apply_absolute_value=True).then_inc(xmax_steps, 1)

            for b in range(BATCH):
                here = range(b * TT, (b + 1) * TT)
                if b < 2:
                    for t in range(TT):
                        row_stats(b, t)
                dve.wait_ge(stats_done, (b + 1) * TT)
                for t in here:
                    dve.bn_aggr(mv[:, t, :], stats[:, t, :]).then_inc(aggr_done, 1)
                y, v = rstd[:, b * TT:(b + 1) * TT], newton[:, 0, b * TT:(b + 1) * TT]
                e = newton[:, 1, b * TT:(b + 1) * TT]
                dve.wait_ge(aggr_done, TT * (b + 1))
                dve.tensor_scalar(v, mv[:, b * TT:(b + 1) * TT, 1], EPS, None, ALU.add).then_inc(rstd_steps, 1)
                meanwhile(b, 0)
                dve.wait_ge(root_done, b + 1)
                dve.reciprocal(y, root[:, b * TT:(b + 1) * TT]).then_inc(rstd_steps, 1)
                meanwhile(b, 1)
                dve.wait_ge(rstd_steps, 5 * b + 2)
                dve.tensor_tensor(e, v, y, ALU.mult).then_inc(rstd_steps, 1)
                meanwhile(b, 2)
                dve.wait_ge(rstd_steps, 5 * b + 3)
                dve.scalar_tensor_tensor(e, e, -0.5, y, ALU.mult, ALU.mult).then_inc(rstd_steps, 1)
                meanwhile(b, 3)
                dve.wait_ge(rstd_steps, 5 * b + 4)
                dve.scalar_tensor_tensor(y, e, 1.5, y, ALU.add, ALU.mult).then_inc(rstd_steps, 1)
                dve.wait_ge(rstd_steps, 5 * b + 5)
                if b >= 2:
                    dve.wait_ge(turned, 2 * (b - 1))
                for t in here:
                    normal(z[:, b % 2, t % TT, :], h[:, t, :], t, z_done)
                if b == 0:
                    dve.wait_ge(wmax_steps, QKV_JOBS)
                    dve.tensor_tensor(wmax[:, :], wmax_p[:, 0, :], wmax_p[:, 1, :], ALU.max).then_inc(wmax_ready, 1)
                    dve.wait_ge(small_in, 16 * 9)
                    dve.tensor_tensor(qkb_s[:, :], qkb[:, :], qk_scale[:, :], ALU.mult).then_inc(qkb_ready, 1)
                else:
                    largest(b - 1)
            largest(BATCH - 1)
            dve.wait_ge(xmax_steps, BATCH)
            dve.tensor_reduce(xmax[:, :], xmax_b[:, :, :], AX.X, ALU.max).then_inc(xmax_ready, 1)
            dve.wait_ge(wpow_ready, 1)
            dve.wait_ge(xpow_ready, 1)
            dve.tensor_tensor(raw[:, :], xpow[:, :], wpow[:, :], ALU.mult).then_inc(cs_steps, 1)
            dve.wait_ge(cs_steps, 1)
            dve.tensor_scalar(raw43[:, :], raw[:, :], FOUR_THIRDS_DOWN, None, ALU.mult).then_inc(cs_steps, 1)
            dve.wait_ge(cs_steps, 2)
            dve.tensor_scalar(cs[:, :].bitcast(U32), raw43[:, :].bitcast(U32), EXPONENT_BITS, None,
                              ALU.bitwise_and).then_inc(cs_steps, 1)
            dve.wait_ge(cs_steps, 3)
            dve.reciprocal(inv[:, :], cs[:, :]).then_inc(cs_steps, 2)
            dve.wait_ge(cs_steps, 5)

            def row_maximum(unit, n, head, t, early=False):
                dve.wait_ge(a_mm, n + 1)
                dve.tensor_reduce(negmax[:, bass.ds(unit, 1), t, head].rearrange("p o -> p o"), ps[:, max_bank(TT * head + t, early), :], AX.X, ALU.max,
                                  negate=True).then_inc(a_read, 1)

            def smooth_lo(b):
                hi, lo, both = X[b % 2]
                tokens = slice(b * SEQ, (b + 1) * SEQ)
                dve.wait_ge(x_hi_done, 2 * b + 1)
                dve.scalar_tensor_tensor(lo[:, :], xT[:, 0, tokens], inv[:, 0:1], hi[:, :].bitcast(F32),
                                         ALU.mult, ALU.subtract).then_inc(x_lo_done, 1)
                dve.wait_ge(x_hi_done, 2 * b + 2)
                dve.scalar_tensor_tensor(both[CB:P, :], xT[CB:P, 1, tokens], inv[CB:P, 1:2],
                                         both[CB:P, :].bitcast(F32), ALU.mult, ALU.subtract).then_inc(x_lo_done, 1)

            dve.wait_ge(w_lo_done, QKV_JOBS)
            for part in qkvT:
                dve.tensor_scalar(part[:, 0, :], part[:, 0, :].bitcast(F32), cs[:, 0:1], None, ALU.mult).then_inc(w_scaled, 1)
            smooth_lo(0)

            def split(b, tile):
                n = QKT * b + tile + 1
                dve.wait_ge(qk_taken, n)
                dve.wait_ge(hi_done, n)
                dve.tensor_tensor(rest[:, tile, :], qk32[:, tile, :], parts[:, b % 2, tile, 0, :], ALU.subtract).then_inc(rest_done, 1)
                dve.wait_ge(rest_done, n)
                dve.tensor_copy(parts[:, b % 2, tile, 1, :], rest[:, tile, :]).then_inc(mid_done, 1)

            def chunk_maximum(chunk):
                for t in range(TT):
                    row_maximum(chunk // HPU, TT * chunk + t, chunk % HPU, t, early=True)

            def early_maxima(n, count):
                for i in range(n, n + count):
                    row_maximum(i // UNIT_BANKS, i, i // TT % HPU, i % TT, early=True)
                return n + count

            early = 0
            for b in range(BATCH):
                if b + 1 < BATCH:
                    smooth_lo(b + 1)
                for tile in range(QKT):
                    split(b, tile)
                    early = early_maxima(early, EARLY[b][tile])
                early = early_maxima(early, sum(EARLY[b][QKT:]))
            early_maxima(early, LEAD * TT - early)

            def normalise(unit):
                o = ps[:, 7, :].rearrange("p (t h c) -> p t h c", t=TT, h=HPU)
                dve.wait_ge(o_turned, 1 + unit + 1)
                dve.reciprocal(rden[:, :, :], o[:, :, :, HD:HD + 1].rearrange("p t h o -> p t (h o)")).then_inc(rden_ready, 1)
                dve.wait_ge(rden_ready, unit + 1)
                dve.tensor_tensor(
                    attn[:, bass.ds(unit, 1), :, :].rearrange("p o t (h d) -> p (o t) h d", d=HD), o[:, :, :, 0:HD],
                    rden[:, :, :].unsqueeze(3).broadcast_to([P, TT, HPU, HD]), ALU.mult).then_inc(attn_ready, 1)

            chunk_maximum(LEAD)
            with dve.Fori(0, UNITS - 2) as unit:
                for n in range(HPU * TT):
                    row_maximum(unit + 2, UNIT_BANKS * (unit + 2) + n, n // TT, n % TT)
                normalise(unit)
            def high(b, buffer, bank, ready, done):
                for c, to in ((0, buffer[0]), (1, buffer[2])):
                    dve.wait_ge(ready, 2 * b + c + 1)
                    dve.tensor_copy(to[:, :], ps[:, bank + c, :]).then_inc(done, 1)

            def low(b, buffer, bank, hi_done, done):
                hi, lo, both = buffer
                dve.wait_ge(hi_done, 2 * b + 1)
                dve.tensor_tensor(lo[:, :], ps[:, bank, :], hi[:, :].bitcast(F32), ALU.subtract).then_inc(done, 1)
                dve.wait_ge(hi_done, 2 * b + 2)
                dve.tensor_tensor(both[CB:P, :], ps[CB:P, bank + 1, :], both[CB:P, :].bitcast(F32),
                                  ALU.subtract).then_inc(done, 1)

            def residual(b, bank):
                for i in range(2):
                    rows = h[:, bass.ds(TT * b + 2 * i, 2), :]
                    dve.wait_ge(proj_mm, 2 * b + i + 1)
                    dve.tensor_tensor(rows, ps[:, bank + i, :].rearrange("p (t c) -> p t c", t=2)[:, :, 0:C], rows,
                                      ALU.add).then_inc(h1_ready, 1)
                wait_apart(dve, h1_ready, 2 * b + 2)
                for t in range(TT):
                    dve.bn_stats(stats[:, t, :], h[:, bass.ds(TT * b + t, 1), :].rearrange("p o c -> p (o c)")).then_inc(stats2, 1)
                wait_apart(dve, stats2, TT * b + TT)
                for t in range(TT):
                    dve.bn_aggr(mv[:, t, :], stats[:, t, :]).then_inc(aggr2, 1)

            def second_norm(b):
                dve.wait_ge(rstd2, b + 1)
                for t in range(TT):
                    normal(z[:, 0, t, :], h[:, bass.ds(TT * b + t, 1), :].rearrange("p o c -> p (o c)"), t, z2_done)

            def split_hidden(b, tiles):
                for m in tiles:
                    dve.wait_ge(gelu_done, FT * b + m + 1)
                    if m in BY_ACT:
                        dve.wait_ge(act_hi, len(BY_ACT) * b + BY_ACT.index(m) + 1)
                    else:
                        dve.tensor_copy(hid[0][:, m, :], hid32[:, m, :]).then_inc(hid_hi, 1)
                        dve.wait_ge(hid_hi, len(BY_DVE) * b + BY_DVE.index(m) + 1)
                    dve.tensor_tensor(hid[1][:, m, :], hid32[:, m, :], hid[0][:, m, :].bitcast(F32),
                                      ALU.subtract).then_inc(hid_lo, 1)

            def result(b, i):
                rows = h[:, bass.ds(TT * b + 2 * i, 2), :]
                dve.wait_ge(f2_mm, 2 * b + i + 1)
                dve.tensor_tensor(rows, ps[:, 6 + i, :].rearrange("p (t c) -> p t c", t=2)[:, :, 0:C], rows,
                                  ALU.add).then_inc(y_ready, 1)

            dve.wait_ge(bias_added, 1)
            high(0, X[0], 0, a_turned, aT_hi)
            low(0, X[0], 0, aT_hi, aT_lo)
            residual(0, 0)
            second_norm(0)
            high(0, X[1], 0, z_turned, zT_hi)
            low(0, X[1], 0, zT_hi, zT_lo)
            normalise(UNITS - 2)
            high(1, X[0], 0, a_turned, aT_hi)
            low(1, X[0], 0, aT_hi, aT_lo)
            residual(1, 0)
            normalise(UNITS - 1)
            with dve.Fori(0, BATCH - 2) as b:
                split_hidden(b, range(2))
                second_norm(b + 1)
                split_hidden(b, range(2, FT))
                low(b + 1, X[1], 0, zT_hi, zT_lo)
                low(b + 2, X[0], 2, aT_hi, aT_lo)
                result(b, 0)
                residual(b + 2, 2)
                result(b, 1)
            split_hidden(BATCH - 2, range(2))
            second_norm(BATCH - 1)
            split_hidden(BATCH - 2, range(2, FT))
            low(BATCH - 1, X[1], 0, zT_hi, zT_lo)
            result(BATCH - 2, 0)
            result(BATCH - 2, 1)
            split_hidden(BATCH - 1, range(FT))
            result(BATCH - 1, 0)
            result(BATCH - 1, 1)

        @block.tensor
        def _(pe):
            mm = pe.matmul

            pe.nop().then_inc(pv_done, KT)
            pe.nop().then_inc(o_turned, 1)
            pe.nop().then_inc(attn_ready, 1)
            pe.nop().then_inc(y_ready, 2)
            pe.nop().then_inc(hid_lo, FT)

            pe.wait_ge(consts, 4)
            def turn_weights(jobs):
                for n in jobs:
                    pe.wait_ge(doubled, (1, 1, 2, 3, 4, 4, 4, 4)[n])
                    if n >= 4:
                        pe.wait_ge(w_hi_done, n - 3)
                    for src, col in weight_jobs[n][2]:
                        rows = src.shape[0]
                        last = pe.transpose(ps[:, 4 + n % 4, col:col + rows], src, ident[0:rows, 0:rows])
                    last.then_inc(w_turned, 1)

            turn_weights(range(4))
            for b in range(BATCH):
                for c in range(2):
                    k = 2 * b + c
                    if c == 0:
                        pe.wait_ge(z_done, TT * (b + 1))
                    else:
                        pe.wait_ge(z_twice, b + 1)
                    if k >= 4:
                        pe.wait_ge(untied, k - 3)
                    for t in range(TT):
                        last = pe.transpose(ps[:, k % 4, t * P:(t + 1) * P],
                                            z[:, b % 2, t, c * P:(c + 1) * P], ident[:, :])
                    last.then_inc(turned, 1)
                turn_weights(WEIGHTS_AFTER[b])

            def scores_for_max(b, g, head, chunk, tiles, early=False, first=False):
                if head == 0 and 0 in tiles:
                    pe.wait_ge(qk_in[g], Q_DMAS * (b + 1))
                for t in tiles:
                    j = TT * head + t
                    if early or j in (0, 1, MAX_SLOT, MAX_SLOT + 1):
                        if not (first and t < 2):
                            pe.wait_ge(a_read, TT * chunk + t - 1)
                    elif j == MAX_SLOT + 2:
                        pe.wait_ge(m_taken, GROUPS * b + g)
                    else:
                        pe.wait_ge(a_read, TT * chunk + t - 2)
                    mm(ps[:, max_bank(j, early), :], QS[g][0:STACK, head, t * P:(t + 1) * P], KS[g][0:STACK, head, :],
                       start=True, stop=True).then_inc(a_mm, 1)

            def turn_max(unit):
                pe.wait_ge(m_parts, 4 * unit + 4)
                if not (isinstance(unit, int) and unit == 0):
                    pe.wait_ge(attn_ready, unit)
                for t in range(TT):
                    last = pe.transpose(ps[0:PARTS * HPU, turned_max_bank(unit), :].bitcast(BF16)[:, t * P:(t + 1) * P],
                                        mparts[:, t, :, :].rearrange("p a h -> p (a h)"), ident16[:, :])
                last.then_inc(m_turned, 1)

            def scores(b, g, kt, step, pairs=range(PAIRS), first=False):
                if kt == 0 and 0 in pairs:
                    pe.wait_ge(m_in[g], M_DMAS * (b + 1))
                for pair in pairs:
                    if not first:
                        pe.wait_ge(p_ready, PAIRS * (step - 1) + pair + 1)
                    for head in (2 * pair, 2 * pair + 1):
                        last = mm(ps[:, 2 + head, :], KS[g][:, head, kt * P:(kt + 1) * P], QS[g][:, head, :],
                                  start=True, stop=True)
                    last.then_inc(b_mm, 1)

            def weigh(unit, g, kt, first=False):
                pe.wait_ge(p_ready, PAIRS * (KT * unit + kt + 1))
                if kt == 0:
                    pe.wait_ge(vu_ready, unit + 1)
                    pe.wait_ge(o_taken, unit)
                for head in range(HPU):
                    last = mm(ps[head * TILE_COLS:(head + 1) * TILE_COLS, 6, :], VU[g][:, kt, head, :],
                              prob[:, kt, head, :], start=kt == 0, stop=kt == KT - 1)
                last.then_inc(pv_done, 1)

            def turn_out(unit):
                pe.wait_ge(o_taken, unit + 1)
                if isinstance(unit, int) and unit == UNITS - 2:
                    pe.wait_ge(m_taken, UNITS)
                elif isinstance(unit, int) and unit == UNITS - 1:
                    pe.wait_ge(attn_ready, UNITS)
                else:
                    pe.wait_ge(a_read, UNIT_BANKS * (unit + 3) - 2)
                for t in range(TT):
                    last = pe.transpose(ps[:, 7, t * P:(t + 1) * P], o_sb[:, t * P:(t + 1) * P], ident[:, :])
                last.then_inc(o_turned, 1)

            def at(b, g, steps):
                return b + (g + steps) // GROUPS, (g + steps) % GROUPS

            def chunk(b, g, ahead, tiles=range(TT), first=False):
                nb, ng = at(b, g, ahead // HPU)
                if isinstance(nb, int) and nb >= BATCH:
                    return
                early = isinstance(b, int) and HPU * (GROUPS * b + g) + ahead <= LEAD
                scores_for_max(nb, ng, ahead % HPU, HPU * (GROUPS * b + g) + ahead, tiles, early, first)

            def step(b, g, kt):
                unit = GROUPS * b + g
                nb, ng = at(b, g, (kt + 1) // KT)
                more = not (isinstance(nb, int) and nb == BATCH)
                if more:
                    scores(nb, ng, (kt + 1) % KT, KT * unit + kt + 1)
                chunk(b, g, LEAD + kt, (0, 1))
                weigh(unit, g, kt)
                if kt == 1 and not (isinstance(b, int) and unit == UNITS - 1):
                    turn_max(unit + 1)
                chunk(b, g, LEAD + kt, (2, 3))

            def turn(rows, bank, done):
                for c in range(2):
                    for t in range(TT):
                        last = pe.transpose(ps[:, bank + c, t * P:(t + 1) * P], rows[:, t, c * P:(c + 1) * P], ident[:, :])
                    last.then_inc(done, 1)

            def turn_attn(b, bank):
                pe.wait_ge(a_copied, 2 * b + 2)
                if bank:
                    pe.wait_ge(h1_ready, 2 * b)
                turn(a_cur, bank, a_turned)

            def turn_z(b):
                pe.wait_ge(z2_twice, b + 1)
                turn(z[:, 0, :, :], 0, z_turned)

            def project(b, bank):
                pe.wait_ge(aT_lo, 2 * b + 2)
                for t in range(TT):
                    for i, (w, c, n) in enumerate(WX):
                        last = mm(ps[:, bank + t // 2, (t % 2) * 256:(t % 2) * 256 + C],
                                  X[0][n][:, t * P:(t + 1) * P], projT[w][:, c, :], start=i == 0, stop=i == 4)
                    if t % 2:
                        last.then_inc(proj_mm, 1)

            def ffn1(b):
                pe.wait_ge(zT_lo, 2 * b + 2)
                for m in range(FT):
                    if m >= 2:
                        pe.wait_ge(gelu_done, FT * b + m - 1)
                    for i, (w, c, n) in enumerate(WX):
                        last = mm(ps[:, 4 + m % 2, :], w1T[w][:, c, m * P:(m + 1) * P], X[1][n][:, :],
                                  start=i == 0, stop=i == 4)
                    last.then_inc(f1_mm, 1)

            def ffn2(b, half):
                pe.wait_ge(y_ready, 2 * b + half + 1)
                pe.wait_ge(attn_ready, 1 + UNITS)
                for t in (2 * half, 2 * half + 1):
                    for m in range(FT):
                        if t == 0:
                            pe.wait_ge(hid_lo, FT + FT * b + m + 1)
                        for w, n in ((0, 0), (0, 1), (1, 0)):
                            last = mm(ps[:, 6 + half, (t % 2) * 256:(t % 2) * 256 + C],
                                      hid[n][:, m, t * P:(t + 1) * P], w2s[w][:, m, :],
                                      start=m + n + w == 0, stop=m == FT - 1 and w == 1)
                last.then_inc(f2_mm, 1)

            def between(step):
                if step == LAST - 6:
                    pe.wait_ge(a_read, TT * HPU * UNITS)
                    turn_attn(0, 0)
                if step == LAST - 5:
                    project(0, 0)
                if step == LAST - 2:
                    turn_z(0)
                if step == LAST - 1:
                    pe.wait_ge(zT_lo, 2)
                    turn_attn(1, 0)
                if step == LAST:
                    project(1, 0)

            def unit_steps(b, g):
                unit = GROUPS * b + g
                final = isinstance(b, int) and unit == UNITS - 1
                for kt in range(1, KT):
                    step(b, g, kt)
                    if isinstance(b, int):
                        between(KT * unit + kt)
                if not final:
                    nb, ng = at(b, g, 1)
                    step(nb, ng, 0)
                    if isinstance(b, int):
                        between(KT * unit + KT)
                turn_out(unit)

            WX = ((0, 0, 0), (0, 0, 1), (1, 0, 0), (0, 1, 2), (1, 1, 2))

            pe.wait_ge(untied, 2 * BATCH)
            pe.wait_ge(w_lo_done, WJ)

            def early_banks(n, count):
                for i in range(n, n + count):
                    chunk(0, 0, i // TT, (i % TT,), first=i < TT)
                return n + count

            early, due = 0, 0
            for b in range(BATCH):
                for tile in range(QKT):
                    if b:
                        pe.wait_ge(hi_done, QKT * (b - 1) + tile + 1)
                    cols = slice(tile * P, (tile + 1) * P)
                    for i, (w, c, n) in enumerate(WX):
                        if b + tile == 0 and i == 0:
                            pe.wait_ge(w_scaled, 2)
                        if b + tile == 0 and i >= 3:
                            pe.wait_ge(far_scaled, w + 1)
                        if tile == 0 and i == 0:
                            pe.wait_ge(x_hi_done, 2 * b + 1)
                        if tile == 0 and i == 1:
                            pe.wait_ge(x_lo_done, 2 * b + 1)
                        if tile == 0 and i == 3:
                            pe.wait_ge(x_lo_done, 2 * b + 2)
                        last = mm(ps[:, 2 + tile, :], qkvT[w][:, c, cols], X[b % 2][n][:, :],
                                  start=i == 0, stop=i == 4)
                    last.then_inc(qk_mm, 1)
                    early, due = early_banks(early, due), EARLY[b][tile]
                for t in range(TT):
                    n = TT * b + t
                    if n >= 3:
                        before = n - 3 if t >= 3 else TT * (b - 1) + (t if t else 3)
                        pe.wait_ge(v_taken, before + 1)
                    tok = slice(t * P, (t + 1) * P)
                    for i, (w, c, x_part) in enumerate(WX):
                        last = mm(ps[:, 5 + t % 3, 0:C], X[b % 2][x_part][:, tok], qkvT[w][:, c, 2 * C:3 * C],
                                  start=i == 0, stop=i == 4)
                    last.then_inc(v_mm, 1)
                    early, due = early_banks(early, due), EARLY[b][QKT + t]
                    if b == BATCH - 1 and t == MAX_AFTER:
                        pe.wait_ge(hi_done, QKT * b + 1)
                        turn_max(0)
            early = early_banks(early, BEFORE_SCORES - early)

            pe.wait_ge(hi_done, QKT * BATCH)
            pe.wait_ge(v_taken, TT * BATCH)
            pe.wait_ge(ones_in, 16 * GROUPS)

            scores(0, 0, 0, 0, first=True)
            early_banks(early, LEAD * TT - early)
            step(0, 0, 0)
            with pe.Fori(0, BATCH - 1) as b:
                for g in range(GROUPS):
                    unit_steps(b, g)
            for g in range(GROUPS):
                unit_steps(BATCH - 1, g)

            pe.wait_ge(w2_lo_done, 1)
            with pe.Fori(0, BATCH - 2) as b:
                ffn1(b)
                turn_z(b + 1)
                turn_attn(b + 2, 2)
                ffn2(b, 0)
                project(b + 2, 2)
                ffn2(b, 1)
            ffn1(BATCH - 2)
            turn_z(BATCH - 1)
            for b in (BATCH - 2, BATCH - 1):
                if b == BATCH - 1:
                    ffn1(b)
                ffn2(b, 0)
                ffn2(b, 1)


_INS = ['x', 'L0_tok_weight', 'L0_attn_qkv_weight', 'L0_attn_qkv_bias', 'L0_attn_proj_weight', 'L0_attn_proj_bias',
        'L0_ffn_in_weight', 'L0_ffn_in_bias', 'L0_ffn_out_weight']


def kernel(**inputs):
    import numpy as _np
    import concourse.bacc as _bacc
    from concourse import mybir as _mybir
    from concourse.bass_utils import run_bass_kernel_spmd as _run

    nc = _bacc.Bacc("TRN2", target_bir_lowering=False, num_devices=1)
    arrays, args = {}, []
    for name in _INS:
        a = _np.ascontiguousarray(inputs[name])
        arrays[f"in_{name}_dram"] = a
        args.append(nc.dram_tensor(f"in_{name}_dram", a.shape, _mybir.dt.from_np(a.dtype), kind="ExternalInput").ap())
    shape = (*inputs['x'].shape, inputs['L0_tok_weight'].shape[1])
    args.append(nc.dram_tensor("out_0_dram", shape, _mybir.dt.float32, kind="ExternalOutput").ap())
    decoder_layer(nc, *args)
    r = _run(nc, [arrays], core_ids=[0])
    return r.results[0]["out_0_dram"]
```
